# Optimizing a Trainium2 kernel written in Bass

```python
import numpy as np
import jax
import jax.numpy as jnp

def _softmax(x, axis=-1):
    return jax.nn.softmax(x, axis=axis)

def _gelu(x):
    return jax.nn.gelu(x, approximate=True)

def _silu(x):
    return jax.nn.silu(x)

def _sigmoid(x):
    return jax.nn.sigmoid(x)

def _layernorm(x, axis=-1, eps=1e-05):
    m = jnp.mean(x, axis=axis, keepdims=True)
    v = jnp.var(x, axis=axis, keepdims=True)
    return (x - m) / jnp.sqrt(v + eps)

def _scatter_add(tgt, idx, src, axis=0):
    return tgt.at[idx].add(src)

def _segment_sum(src, seg, n):
    return jax.ops.segment_sum(src, seg, n)
kernel_name = 'mk_gnn_preln_d1_gnn_r8_b1e2e4'

def setup_inputs(seed: int=0):
    np.random.seed(seed)
    _w = jnp.asarray

    def _rec_inputs():
        import jax
        import jax.numpy as jnp
        _gk = jax.random.key(seed)
        x = -0.000202 + 1 * jax.random.normal(jax.random.fold_in(_gk, 1), (6250, 128), jnp.float32)
        src = jax.random.randint(jax.random.fold_in(_gk, 2), (200000,), 0, 6250, jnp.int32)
        dst = jax.random.randint(jax.random.fold_in(_gk, 3), (200000,), 0, 6250, jnp.int32)
        _o = jnp.argsort(dst, stable=True)
        src = src[_o]
        dst = dst[_o]
        edge_attr_64 = 0.000196303 + 1.00016 * jax.random.normal(jax.random.fold_in(_gk, 11), (200000, 64), jnp.float32)
        return (x, src, dst, edge_attr_64)
    x, src, dst, edge_attr_64 = _rec_inputs()

    def _L0_gnn_setup():
        import jax, jax.numpy as jnp
        import numpy as np
        N, E = (6250, 50000)
        NODE_DIM, EDGE_DIM = (128, 64)
        MSG_IN = 2 * NODE_DIM + EDGE_DIM
        key = jax.random.key(seed)
        ks = jax.random.split(key, 12)
        h = jax.random.normal(ks[0], (N, NODE_DIM), dtype=jnp.float32)
        edge_index = jax.random.randint(ks[1], (2, E), 0, N, dtype=jnp.int64)
        e = jax.random.normal(ks[2], (E, EDGE_DIM), dtype=jnp.float32)

        def lin(k, fan_in, fan_out):
            bound = 1.0 / np.sqrt(fan_in)
            k1, k2 = jax.random.split(k)
            w = jax.random.uniform(k1, (fan_in, fan_out), minval=-bound, maxval=bound, dtype=jnp.float32)
            b = jax.random.uniform(k2, (fan_out,), minval=-bound, maxval=bound, dtype=jnp.float32)
            return (w, b)
        w1, b1 = lin(ks[3], MSG_IN, NODE_DIM)
        w2, b2 = lin(ks[4], NODE_DIM, NODE_DIM)
        wg, bg = lin(ks[5], MSG_IN, NODE_DIM)
        wu, bu = lin(ks[6], 2 * NODE_DIM, NODE_DIM)
        return {'h': h, 'edge_index': edge_index, 'e': e, 'w1': w1, 'b1': b1, 'w2': w2, 'b2': b2, 'wg': wg, 'bg': bg, 'wu': wu, 'bu': bu}
    _L0_gnn_all = _L0_gnn_setup()
    _L0_gnn_in = {k: v for k, v in _L0_gnn_all.items() if k in ('w1', 'b1', 'w2', 'b2', 'wg', 'bg', 'wu', 'bu')}
    del _L0_gnn_all
    return {'x': x, 'src': src, 'dst': dst, 'edge_attr_64': edge_attr_64, 'L0_gnn_w1': _L0_gnn_in['w1'], 'L0_gnn_b1': _L0_gnn_in['b1'], 'L0_gnn_w2': _L0_gnn_in['w2'], 'L0_gnn_b2': _L0_gnn_in['b2'], 'L0_gnn_wg': _L0_gnn_in['wg'], 'L0_gnn_bg': _L0_gnn_in['bg'], 'L0_gnn_wu': _L0_gnn_in['wu'], 'L0_gnn_bu': _L0_gnn_in['bu']}

def reference(x, src, dst, edge_attr_64, L0_gnn_w1, L0_gnn_b1, L0_gnn_w2, L0_gnn_b2, L0_gnn_wg, L0_gnn_bg, L0_gnn_wu, L0_gnn_bu):
    import jax
    import jax.numpy as jnp

    def _L0_gnn_ref(h, edge_index, e, w1, b1, w2, b2, wg, bg, wu, bu):
        import jax, jax.numpy as jnp
        import numpy as np
        N, E = (6250, 50000)
        NODE_DIM, EDGE_DIM = (128, 64)
        MSG_IN = 2 * NODE_DIM + EDGE_DIM
        src, dst = (edge_index[0], edge_index[1])
        msg_in = jnp.concatenate([h[src], h[dst], e], axis=-1)
        messages = jax.nn.silu(msg_in @ w1 + b1) @ w2 + b2
        gates = jax.nn.sigmoid(msg_in @ wg + bg)
        messages = messages * gates
        n = h.shape[0]
        agg = jax.ops.segment_sum(messages, dst, num_segments=n)
        deg = jax.ops.segment_sum(jnp.ones((dst.shape[0],), h.dtype), dst, num_segments=n)
        agg = agg / jnp.maximum(deg, 1.0)[:, None]
        h_new = jax.nn.silu(jnp.concatenate([h, agg], axis=-1) @ wu + bu)
        return h_new
    edge_index = jnp.stack([src, dst])
    h = jnp.maximum(_layernorm(x, axis=-1), 0.0)
    x = x + _L0_gnn_ref(h, edge_index, edge_attr_64, L0_gnn_w1, L0_gnn_b1, L0_gnn_w2, L0_gnn_b2, L0_gnn_wg, L0_gnn_bg, L0_gnn_wu, L0_gnn_bu)
    return x

_drawn_inputs = setup_inputs


def setup_inputs(seed=0):
    import zlib

    import numpy as np

    out = dict(_drawn_inputs(seed))
    spreads = {}
    factors = {'edge_attr_64': 8.0,
     'L0_gnn_w1': 5.781,
     'L0_gnn_b1': 8.0,
     'L0_gnn_w2': 6.419,
     'L0_gnn_b2': 8.0,
     'L0_gnn_wg': 8.0,
     'L0_gnn_bg': 26.633,
     'L0_gnn_bu': 3.366}
    for name, (base, spread) in spreads.items():
        noise = np.random.default_rng([zlib.crc32(name.encode()), seed]).standard_normal(out[name].shape)
        drawn = base * np.exp(spread * noise) if base else spread * noise
        out[name] = jnp.asarray(drawn.astype(out[name].dtype))
    for name, factor in factors.items():
        out[name] = (out[name] * factor).astype(out[name].dtype)
    return out
```

```python
import concourse.bass as bass
from concourse import mybir
from contextlib import ExitStack

N, E, D, ED = 6250, 200000, 128, 64
P = 128
TILES = 8
HALF = TILES // 2
CHUNK = TILES * P
CHUNKS = -(-E // CHUNK)
REPEATED = CHUNKS * CHUNK - E
ROUNDS = CHUNKS // 2
WINDOW = 64
LAST_BASE = N - WINDOW
NTILES = -(-N // P)
NODE_REPEATED = NTILES * P - N
WIDE = 512
WIDES = -(-N // WIDE)
NPAD = WIDES * WIDE
FOREIGN = -1.0e6
EPS = 1e-5
GROUP = 7
NGROUPS = NTILES // GROUP
assert CHUNKS % 2 == 0 and NTILES % GROUP == 0


def node_start(t):
    return min(t * P, N - P)


def gnn_program(nc, x, src_ch, dst_rows, dst_cols, dst_first, e_ch, w1, b1, w2, b2, wg, bg, wu, bu, out):
    fp32, bf16, i32 = mybir.dt.float32, mybir.dt.bfloat16, mybir.dt.int32
    ALU = mybir.AluOpType
    ACT = mybir.ActivationFunctionType
    AX = mybir.AxisListType.X
    ds = bass.ds

    src_table = nc.dram_tensor("src_table", [N, 2 * D], fp32, kind="Internal").ap()
    dst_table = nc.dram_tensor("dst_table", [N, 2 * D], fp32, kind="Internal").ap()
    src_rows2 = src_ch.rearrange("c p t -> (c p) t")
    e_rows = e_ch.rearrange("c f n -> (c f) n")

    ctx = ExitStack()
    with ctx:
        def sb(name, shape, dt=fp32):
            return ctx.enter_context(nc.sbuf_tensor(name, shape, dt))

        def pb(name, shape):
            return ctx.enter_context(nc.psum_tensor(name, shape, fp32))

        def sem(name):
            return ctx.enter_context(nc.semaphore(name))

        xs = sb("xs", [P, NTILES, D])
        hT = sb("hT", [P, NTILES, P])
        sums = sb("sums", [P, 2, NPAD])
        h = sums[:, 0, 0:NTILES * D].rearrange("p (t d) -> p t d", d=D)
        squares = sums[:, 1, 0:NTILES * D].rearrange("p (t d) -> p t d", d=D)
        stat = sb("stat", [P, 3, NTILES])
        w_node = sb("w_node", [P, 4 * D])
        bias_dst = sb("bias_dst", [P, 2 * D])
        bias_up = sb("bias_up", [P, D])
        w2_sb = sb("w2_sb", [P, D])
        wu_sb = sb("wu_sb", [P, 2, D])
        b2_all = sb("b2_all", [P, 2, D])
        b2_parts = sb("b2_parts", [P, HALF, D], bf16)
        ident = sb("ident", [P, P])
        ones_bf = sb("ones_bf", [P, P], bf16)
        ones = sb("ones", [P, P])
        iota_i = sb("iota_i", [P, WIDE], i32)
        iota_f = sb("iota_f", [P, WIDE])
        row_i = sb("row_i", [P, 1], i32)
        row_f = sb("row_f", [P, 1])
        dcol_i = sb("dcol_i", [P, CHUNKS * TILES], i32)
        dcol = sb("dcol", [P, CHUNKS * TILES])
        drel = sb("drel", [P, CHUNKS * TILES])
        first_i = sb("first_i", [P, CHUNKS], i32)
        base_i = sb("base_i", [P, CHUNKS], i32)
        base_f = sb("base_f", [P, CHUNKS])
        own_node = sb("own_node", [P, CHUNKS])
        outside = sb("outside", [P, 2])
        flag_i = sb("flag_i", [1, 1], i32)
        lhs = [sb(f"lhs{k}", [P, CHUNK]) for k in range(2)]
        rhs = [sb(f"rhs{k}", [P, 2 * D]) for k in range(2)]
        dst_row = [sb(f"dst_row{k}", [P, CHUNK], i32) for k in range(2)]
        idx = [sb(f"idx{k}", [P, TILES], i32) for k in range(2)]
        gath = [sb(f"gath{k}", [P, TILES, 2 * D]) for k in range(2)]
        z = [sb(f"z{k}", [P, HALF, 2 * D]) for k in range(2)]
        sig = [sb(f"sig{k}", [P, HALF, 2 * D]) for k in range(2)]
        act_in = [sb(f"a{k}", [P, HALF, D]) for k in range(2)]
        act_T = [sb(f"aT{k}", [P, HALF * P]) for k in range(2)]
        msg = [sb(f"msg{k}", [P, HALF, D]) for k in range(2)]
        hot = [sb(f"hot{k}", [P, TILES, WINDOW]) for k in range(2)]
        hot_bf = [sb(f"hot_bf{k}", [P, TILES, WINDOW], bf16) for k in range(2)]
        stage = [gath[k // 4].rearrange("p t c -> p (t c)")[:, (k % 4) * 512:(k % 4 + 1) * 512] for k in range(8)]

        zp = [pb(f"zp{k}", [P, HALF * 2 * D]) for k in range(2)]
        tp = pb("tp", [P, 512])
        mp = [pb(f"mp{k}", [P, 512]) for k in range(2)]
        sp_ = pb("sum_p", [P, 512])

        x_in = sem("x_in")
        w_in = sem("w_in")
        d_in = sem("d_in")
        ready = sem("ready")
        iota_made = sem("iota_made")
        v = sem("v")
        centred = sem("centred")
        squared = sem("squared")
        var_done = sem("var_done")
        dev_done = sem("dev_done")
        h_done = sem("h_done")
        t_done = sem("t_done")
        ht_done = sem("ht_done")
        tab_done = sem("tab_done")
        staged_src = sem("staged_src")
        staged_dst = sem("staged_dst")
        stored = [sem(f"stored{k}") for k in range(8)]
        outside_done = sem("outside_done")
        outside_sum = sem("outside_sum")
        flag_done = sem("flag_done")
        N_W = 14

        with nc.Block() as block:

            @block.sync
            def _(sp):
                for g in range(NGROUPS):
                    t0, t1 = g * GROUP, (g + 1) * GROUP
                    whole = min(t1, N // P)
                    sp.dma_start(xs[:, t0:whole, :], x[t0 * P:whole * P, :].rearrange("(t p) d -> p t d", p=P)) \
                        .then_inc(x_in, 16)
                sp.dma_start(xs[:, NTILES - 1, :], x[N - P:N, :]).then_inc(x_in, 16)
                for t in range(NTILES):
                    skip = NODE_REPEATED if t == NTILES - 1 else 0
                    n0 = node_start(t)
                    sp.wait_ge(staged_src, t + 1)
                    sp.dma_start(src_table[n0 + skip:n0 + P, :], stage[t % 8][skip:P, 0:2 * D]).then_inc(stored[t % 8], 16)
                    sp.wait_ge(staged_dst, t + 1)
                    sp.dma_start(dst_table[n0 + skip:n0 + P, :], stage[t % 8][skip:P, 2 * D:4 * D]) \
                        .then_inc(stored[t % 8], 16)
                for k in range(8):
                    sp.wait_ge(stored[k], 32 * len(range(k, NTILES, 8)))

            @block.gpsimd
            def _(pool):
                pool.memset(ident[:, :], 0.0).then_inc(iota_made, 1)
                pool.wait_ge(iota_made, 1)
                pool.affine_select(out=ident[:, :], in_=ident[:, :], compare_op=ALU.not_equal, fill=1.0,
                                   base=0, pattern=[[-1, P]], channel_multiplier=1).then_inc(ready, 1)
                pool.memset(ones_bf[:, :], 1.0).then_inc(ready, 1)
                pool.memset(ones[:, :], 1.0).then_inc(ready, 1)
                pool.iota(iota_i[:, :], pattern=[[1, WIDE]], base=0, channel_multiplier=0).then_inc(ready, 1)
                pool.iota(row_i[:, :], pattern=[[0, 1]], base=-WINDOW, channel_multiplier=1).then_inc(ready, 1)
                pool.memset(b2_parts[:, :, :], 0.0).then_inc(ready, 1)

            @block.scalar
            def _(act):
                for k, w in enumerate((w1, wg)):
                    act.dma_start(w_node[:, k * D:(k + 1) * D], w[0:D, :]).then_inc(w_in, 16)
                    act.dma_start(w_node[:, (2 + k) * D:(3 + k) * D], w[D:2 * D, :]).then_inc(w_in, 16)
                    for r in rhs:
                        act.dma_start(r[0:ED, k * D:(k + 1) * D], w[2 * D:2 * D + ED, :]).then_inc(w_in, 16)
                act.dma_start(bias_dst[:, 0:D], b1[None, :].to_broadcast([P, D])).then_inc(w_in, 16)
                act.dma_start(bias_dst[:, D:2 * D], bg[None, :].to_broadcast([P, D])).then_inc(w_in, 16)
                act.dma_start(bias_up[:, :], bu[None, :].to_broadcast([P, D])).then_inc(w_in, 16)
                act.dma_start(b2_all[:, 0, :], b2[None, :].to_broadcast([P, D])).then_inc(w_in, 16)
                act.dma_start(w2_sb[:, :], w2[:, :]).then_inc(w_in, 16)
                act.dma_start(wu_sb[:, :, :], wu.rearrange("(k p) d -> p k d", p=P)).then_inc(w_in, 16)
                act.dma_start(dcol_i[:, :], dst_cols[:, :]).then_inc(d_in, 16)
                act.dma_start(first_i[:, :], dst_first[:, :].to_broadcast([P, CHUNKS])).then_inc(d_in, 16)
                for g in range(NGROUPS):
                    act.wait_ge(centred, g + 1)
                    s = slice(g * GROUP, (g + 1) * GROUP)
                    nc.scalar.activation(squares[:, s, :], h[:, s, :], ACT.Square).then_inc(squared, 1)
                for g in range(NGROUPS):
                    act.wait_ge(var_done, g + 1)
                    s = slice(g * GROUP, (g + 1) * GROUP)
                    nc.scalar.activation(stat[:, 2, s], stat[:, 1, s], ACT.Sqrt).then_inc(dev_done, 1)
                for t in range(NTILES):
                    act.wait_ge(t_done, t + 1)
                    nc.scalar.copy(hT[:, t, :], tp[:, 0:P]).then_inc(ht_done, 1)
                    act.wait_ge(tab_done, t + 1)
                    if t >= 8:
                        act.wait_ge(stored[t % 8], 32 * (t // 8))
                    nc.scalar.copy(stage[t % 8][:, 0:2 * D], zp[t % 2][:, 0:2 * D]).then_inc(staged_src, 1)

            @block.vector
            def _(dve):
                links = [0]

                def link(ins):
                    links[0] += 1
                    ins.then_inc(v, 1)
                    dve.wait_ge(v, links[0])

                for g in range(NGROUPS):
                    dve.wait_ge(x_in, 16 * (NGROUPS + 1))
                    s = slice(g * GROUP, (g + 1) * GROUP)
                    link(nc.vector.tensor_reduce(stat[:, 0, s], xs[:, s, :], AX, ALU.add))
                    link(nc.vector.tensor_scalar(stat[:, 0, s], stat[:, 0, s], 1.0 / D, None, ALU.mult))
                    nc.vector.tensor_tensor(h[:, s, :], xs[:, s, :],
                                            stat[:, 0, s].unsqueeze(2).to_broadcast([P, GROUP, D]),
                                            ALU.subtract).then_inc(centred, 1)
                for g in range(NGROUPS):
                    dve.wait_ge(squared, g + 1)
                    s = slice(g * GROUP, (g + 1) * GROUP)
                    link(nc.vector.tensor_reduce(stat[:, 1, s], squares[:, s, :], AX, ALU.add))
                    nc.vector.tensor_scalar(stat[:, 1, s], stat[:, 1, s], 1.0 / D, EPS, ALU.mult, ALU.add) \
                        .then_inc(var_done, 1)
                    dve.wait_ge(dev_done, g + 1)
                    link(nc.vector.reciprocal(stat[:, 2, s], stat[:, 2, s]))
                    nc.vector.scalar_tensor_tensor(out=h[:, s, :], in0=h[:, s, :], scalar=0.0,
                                                   in1=stat[:, 2, s].unsqueeze(2).to_broadcast([P, GROUP, D]),
                                                   op0=ALU.max, op1=ALU.mult).then_inc(h_done, 1)
                dve.wait_ge(w_in, 16 * N_W)
                dve.wait_ge(ready, 6)
                dve.wait_ge(d_in, 32)

                link(nc.vector.tensor_scalar(base_f[:, :], first_i[:, :], float(LAST_BASE), None, ALU.min))
                nc.vector.tensor_copy(base_i[:, :], base_f[:, :])
                nc.vector.tensor_copy(iota_f[:, :], iota_i[:, :])
                link(nc.vector.tensor_copy(row_f[:, :], row_i[:, :]))
                nc.vector.tensor_scalar(own_node[:, :], base_f[:, :], row_f[:, 0:1], None, ALU.add)
                link(nc.vector.tensor_copy(dcol[:, :], dcol_i[:, :]))
                link(nc.vector.tensor_tensor(drel[:, :].rearrange("p (c t) -> p c t", t=TILES),
                                             dcol[:, :].rearrange("p (c t) -> p c t", t=TILES),
                                             base_f[:, :].unsqueeze(2).to_broadcast([P, CHUNKS, TILES]), ALU.subtract))
                lo = nc.vector.tensor_reduce(outside[:, 0:1], drel[:, :], AX, ALU.min)
                link(lo)
                link(nc.vector.tensor_reduce(outside[:, 1:2], drel[:, :], AX, ALU.max))
                link(nc.vector.tensor_scalar(outside[:, 0:1], outside[:, 0:1], 0.0, None, ALU.is_lt))
                nc.vector.tensor_scalar(outside[:, 1:2], outside[:, 1:2], float(WINDOW - 1), None, ALU.is_gt) \
                    .then_inc(outside_done, 1)
                c0 = (CHUNKS - 1) * TILES
                full, rest = REPEATED // P, REPEATED % P
                dve.wait_ge(v, links[0])
                for m in (drel, dcol):
                    link(nc.vector.memset(m[:, c0:c0 + full], FOREIGN))
                    if rest:
                        link(nc.vector.memset(m[0:rest, c0 + full:c0 + full + 1], FOREIGN))
                link(nc.vector.tensor_copy(b2_parts[0:1, 0, :], b2_all[0:1, 0, :]))
                for row in (WINDOW // 2, WINDOW):
                    r = slice(row, row + 1)
                    link(nc.vector.tensor_copy(b2_parts[r, 0, :], b2_all[r, 0, :]))
                    link(nc.vector.tensor_tensor(b2_all[r, 1, :], b2_all[r, 0, :], b2_parts[r, 0, :], ALU.subtract))
                    link(nc.vector.tensor_copy(b2_parts[r, 0, :], b2_all[r, 1, :]))
                r = slice(WINDOW, WINDOW + 1)
                link(nc.vector.tensor_tensor(b2_all[r, 0, :], b2_all[r, 1, :], b2_parts[r, 0, :], ALU.subtract))
                link(nc.vector.tensor_copy(b2_parts[r, 0, :], b2_all[r, 0, :]))
                for j in range(1, HALF):
                    link(nc.vector.tensor_copy(b2_parts[0:96, j, :], b2_parts[0:96, 0, :]))
                for t in range(NTILES):
                    dve.wait_ge(staged_src, t + 1)
                    nc.vector.tensor_tensor(stage[t % 8][:, 2 * D:4 * D], zp[t % 2][:, 2 * D:4 * D], bias_dst[:, :],
                                            ALU.add).then_inc(staged_dst, 1)
                dve.wait_ge(outside_sum, 1)
                nc.vector.tensor_copy(flag_i[:, :], mp[0][0:1, 0:1]).then_inc(flag_done, 1)
                dve.wait_ge(t_done, NTILES)
                nc.vector.memset(sums[:, :, :], 0.0)

            @block.tensor
            def _(pe):
                pe.wait_ge(ready, 6)
                pe.wait_ge(w_in, 16 * N_W)
                for t in range(NTILES):
                    if t % GROUP == 0:
                        pe.wait_ge(h_done, t // GROUP + 1)
                    if t >= 1:
                        pe.wait_ge(ht_done, t)
                    nc.tensor.transpose(tp[:, 0:P], h[:, t, :], ident[:, :]).then_inc(t_done, 1)
                    pe.wait_ge(ht_done, t + 1)
                    if t >= 2:
                        pe.wait_ge(staged_dst, t - 1)
                    nc.tensor.matmul(zp[t % 2][:, 0:512], hT[:, t, :], w_node[:, :], start=True, stop=True) \
                        .then_inc(tab_done, 1)
                pe.wait_ge(outside_done, 1)
                nc.tensor.matmul(mp[0][0:1, 0:1], outside[:, 0:1], ones[:, 0:1], start=True, stop=False)
                nc.tensor.matmul(mp[0][0:1, 0:1], outside[:, 1:2], ones[:, 0:1], start=False, stop=True) \
                    .then_inc(outside_sum, 1)

        lhs_in = [sem(f"lhs_in{k}") for k in range(2)]
        dst_in = [sem(f"dst_in{k}") for k in range(2)]
        idx_in = [sem(f"idx_in{k}") for k in range(2)]
        gathered = [sem(f"gathered{j}") for j in range(4)]
        opened = sem("opened")
        hotT_done = sem("hotT_done")
        hot_done = sem("hot_done")
        hot_bf_done = sem("hot_bf_done")
        z_done = sem("z_done")
        z_sum = sem("z_sum")
        sig_done = sem("sig_done")
        a_done = sem("a_done")
        tr_done = sem("tr_done")
        aT_done = sem("aT_done")
        w2_done = sem("w2_done")
        msg_done = sem("msg_done")
        added = sem("added")
        sums_done = sem("sums_done")

        g_start = sem("g_start")
        g_in = sem("g_in")
        g_rows = sem("g_rows")
        g_z = sem("g_z")
        g_zs = sem("g_zs")
        g_sig = sem("g_sig")
        g_a = sem("g_a")
        g_t = sem("g_t")
        g_aT = sem("g_aT")
        g_w2 = sem("g_w2")
        g_msg = sem("g_msg")
        g_hot = sem("g_hot")
        g_sum = sem("g_sum")
        g_v = sem("g_v")
        g_windows = sem("g_windows")
        gdst = dst_row[0][:, 0:TILES]
        iota_w = iota_f[:, :]
        hot_w = hot[1].rearrange("p t n -> p (t n)")[:, 0:WIDE]
        rel_w = [outside[:, 0:1], outside[:, 1:2]]

        def branches(eng, general, windowed):
            general_case = eng.value_load(flag_i[0:1, 0:1], min_val=0, max_val=2 * P)
            with eng.If(general_case > 0):
                general()
            with eng.Else():
                windowed()
            eng.nop()

        with nc.Block() as block:

            @block.sync
            def _(sp):
                def windowed():
                    def load(i, k, first):
                        c = 2 * i + k
                        if not first:
                            for j in (2 * k, 2 * k + 1):
                                sp.wait_ge(gathered[j], 64 * i)
                        sp.dma_start(idx[k][:, :], src_rows2[ds(c * P, P), :]).then_inc(idx_in[k], 16)
                        if not first:
                            sp.wait_ge(z_done, 2 * c - 2)
                        base = sp.value_load(base_i[0:1, ds(c, 1)], min_val=0, max_val=LAST_BASE)
                        sp.dma_start(dst_row[k][WINDOW:P, :], dst_rows[ds(c, 1), :].to_broadcast([WINDOW, CHUNK])) \
                            .then_inc(dst_in[k], 16)
                        sp.dma_start(rhs[k][WINDOW:P, :], dst_table[ds(base, WINDOW), :]).then_inc(lhs_in[k], 16)
                        sp.dma_start(lhs[k][0:ED, :], e_rows[ds(c * ED, ED), :]).then_inc(lhs_in[k], 16)

                    for k in range(2):
                        load(0, k, True)
                    with sp.Fori(1, ROUNDS) as i:
                        for k in range(2):
                            load(i, k, False)

                def general():
                    with sp.Fori(0, CHUNKS) as c:
                        sp.wait_ge(g_start, TILES * c + 1)
                        sp.dma_start(idx[0][:, :], src_rows2[ds(c * P, P), :]).then_inc(g_in, 16)
                        sp.dma_start(gdst, dst_cols[:, ds(c * TILES, TILES)]).then_inc(g_in, 16)
                        sp.dma_start(lhs[0][0:ED, :], e_rows[ds(c * ED, ED), :]).then_inc(g_in, 16)

                branches(sp, general, windowed)

            @block.gpsimd
            def _(pool):
                def gather(table, to, index):
                    return pool.indirect_dma_start(out=to, out_offset=None, in_=table[:, :],
                                                   in_offset=bass.IndirectOffsetOnAxis(ap=index, axis=0))

                def windowed():
                    def gathers(i, first):
                        for j in range(4):
                            k, h0 = j // 2, (j % 2) * HALF
                            if h0 == 0:
                                pool.wait_ge(idx_in[k], 16 * (i + 1))
                            if not first:
                                pool.wait_ge(z_sum, 4 * i + j - 3)
                            pool.sem_inc(opened, 1)
                            for t in range(h0, h0 + HALF):
                                pool.indirect_dma_start(
                                    out=gath[k][:, t, :], out_offset=None, in_=src_table[:, :],
                                    in_offset=bass.IndirectOffsetOnAxis(ap=idx[k][:, t:t + 1], axis=0)).then_inc(gathered[j], 16)

                    gathers(0, True)
                    with pool.Fori(1, ROUNDS) as i:
                        gathers(i, False)

                def general():
                    pool.sem_inc(g_start, 1)
                    with pool.Fori(0, CHUNKS) as c:
                        pool.wait_ge(g_in, 48 * (c + 1))
                        for t in range(TILES):
                            pool.wait_ge(g_start, TILES * c + t + 1)
                            pool.sem_inc(opened, 1)
                            gather(src_table, gath[0][:, 0, :], idx[0][:, t:t + 1]).then_inc(g_rows, 16)
                            gather(dst_table, gath[0][:, 1, :], gdst[:, t:t + 1]).then_inc(g_rows, 16)

                branches(pool, general, windowed)

            @block.scalar
            def _(act):
                def windowed():
                    def half(s, c, j, first):
                        b = j % 2
                        act.wait_ge(z_sum, s + 1)
                        if not first:
                            act.wait_ge(msg_done, s - 1)
                        nc.scalar.activation(sig[b][:, :, :], z[b][:, :, :], ACT.Sigmoid).then_inc(sig_done, 1)
                        if b == 0:
                            k = j // 2
                            act.wait_ge(hot_done, c + 1)
                            if not first:
                                act.wait_ge(added, 2 * c - 2)
                            nc.scalar.copy(hot_bf[k][:, :, :], hot[k][:, :, :]).then_inc(hot_bf_done, 1)
                        act.wait_ge(tr_done, s + 1)
                        if not first:
                            act.wait_ge(w2_done, s - 1)
                        nc.scalar.copy(act_T[b][:, :], tp[:, :]).then_inc(aT_done, 1)

                    for j in range(4):
                        half(j, j // 2, j, j < 2)
                    with act.Fori(1, ROUNDS) as i:
                        for j in range(4):
                            half(4 * i + j, 2 * i + j // 2, j, False)

                def general():
                    with act.Fori(0, CHUNKS) as c:
                        for t in range(TILES):
                            n = TILES * c + t + 1
                            act.wait_ge(g_zs, n)
                            nc.scalar.activation(sig[0][:, 0, :], z[0][:, 0, :], ACT.Sigmoid).then_inc(g_sig, 1)
                            act.wait_ge(g_t, n)
                            nc.scalar.copy(act_T[0][:, 0:P], tp[:, 0:P]).then_inc(g_aT, 1)

                branches(act, general, windowed)

            @block.vector
            def _(dve):
                def windowed():
                    def hot_rows(c, k, round_end, first):
                        dve.wait_ge(dst_in[k], 16 * round_end)
                        if not first:
                            dve.wait_ge(z_done, 2 * c - 2)
                        nc.vector.tensor_scalar(lhs[k][WINDOW:P, :], dst_row[k][WINDOW:P, :],
                                                own_node[WINDOW:P, ds(c, 1)], None, ALU.is_equal) \
                            .then_inc(hotT_done, 1)

                    def hot_cols(c, k, first):
                        if not first:
                            dve.wait_ge(added, 2 * c - 2)
                            dve.wait_ge(hot_bf_done, c - 1)
                        nc.vector.tensor_tensor(
                            hot[k][:, :, :], iota_f[:, 0:WINDOW].unsqueeze(1).to_broadcast([P, TILES, WINDOW]),
                            drel[:, ds(c * TILES, TILES)].unsqueeze(2).to_broadcast([P, TILES, WINDOW]),
                            ALU.is_equal).then_inc(hot_done, 1)

                    def z_add(s, j, round_end, first):
                        b = j % 2
                        dve.wait_ge(z_done, s + 1)
                        dve.wait_ge(gathered[j], 64 * round_end)
                        if not first:
                            dve.wait_ge(sig_done, s - 1)
                            dve.wait_ge(a_done, s - 1)
                        nc.vector.tensor_tensor(
                            z[b][:, :, :], zp[b][:, :].rearrange("p (t c) -> p t c", t=HALF),
                            gath[j // 2][:, b * HALF:(b + 1) * HALF, :], ALU.add).then_inc(z_sum, 1)

                    def a_mul(s, j, first):
                        b = j % 2
                        dve.wait_ge(sig_done, s + 1)
                        if not first:
                            dve.wait_ge(tr_done, s - 1)
                        nc.vector.tensor_tensor(act_in[b][:, :, :], z[b][:, :, 0:D], sig[b][:, :, 0:D],
                                                ALU.mult).then_inc(a_done, 1)

                    def gate(s, j, first):
                        b = j % 2
                        dve.wait_ge(w2_done, s + 1)
                        dve.wait_ge(sig_done, s + 1)
                        if not first:
                            dve.wait_ge(added, s - 1)
                        nc.vector.tensor_tensor(msg[b][:, :, :], mp[b][:, :].rearrange("p (t c) -> p t c", t=HALF),
                                                sig[b][:, :, D:2 * D], ALU.mult).then_inc(msg_done, 1)

                    def add_window(c):
                        dve.wait_ge(added, 2 * c + 2)
                        base = dve.value_load(base_i[0:1, ds(c, 1)], min_val=0, max_val=LAST_BASE)
                        to = sums[:, :, ds(base, WINDOW)]
                        if not (isinstance(c, int) and c == 0):
                            dve.wait_ge(sums_done, c)
                        nc.vector.tensor_tensor(to, to, sp_[:, 0:2 * WINDOW].rearrange("p (k n) -> p k n", k=2),
                                                ALU.add).then_inc(sums_done, 1)

                    def steps(i, first=False, last=False):
                        for j in range(4):
                            s, c = 4 * i + j, 2 * i + j // 2
                            ahead = j == 1 or (j == 3 and not last)
                            z_add(s, j, i + 1, first and j < 2)
                            if ahead:
                                hot_rows(c + 1, (j // 2 + 1) % 2, i + 1 + j // 2, first and j == 1)
                            if not (first and j == 0):
                                gate(s - 1, (j - 1) % 4, first and j <= 2)
                            a_mul(s, j, first and j < 2)
                            if j % 2 and not (first and j == 1):
                                add_window(c - 1)
                            if ahead:
                                hot_cols(c + 1, (j // 2 + 1) % 2, first and j == 1)

                    hot_rows(0, 0, 1, True)
                    hot_cols(0, 0, True)
                    steps(0, first=True)
                    with dve.Fori(1, ROUNDS - 1) as i:
                        steps(i)
                    steps(ROUNDS - 1, last=True)
                    gate(4 * ROUNDS - 1, 3, False)
                    add_window(CHUNKS - 1)

                def general():
                    with dve.Fori(0, CHUNKS) as c:
                        for t in range(TILES):
                            n = TILES * c + t + 1
                            dve.wait_ge(g_z, n)
                            dve.wait_ge(g_rows, 32 * n)
                            nc.vector.tensor_tensor(z[0][:, 1, :], zp[0][:, 0:2 * D], gath[0][:, 0, :], ALU.add) \
                                .then_inc(g_v, 1)
                            dve.wait_ge(g_v, (WIDES + 2) * (n - 1) + 1)
                            nc.vector.tensor_tensor(z[0][:, 0, :], z[0][:, 1, :], gath[0][:, 1, :], ALU.add) \
                                .then_inc(g_zs, 1)
                            dve.wait_ge(g_sig, n)
                            nc.vector.tensor_tensor(act_in[0][:, 0, :], z[0][:, 0, 0:D], sig[0][:, 0, 0:D], ALU.mult) \
                                .then_inc(g_a, 1)
                            dve.wait_ge(g_w2, n)
                            nc.vector.tensor_tensor(msg[0][:, 0, :], mp[0][:, 0:D], sig[0][:, 0, D:2 * D], ALU.mult) \
                                .then_inc(g_msg, 1)
                            nc.vector.tensor_copy(rel_w[0], dcol[:, ds(c * TILES + t, 1)]).then_inc(g_v, 1)
                            with dve.Fori(0, WIDES) as w:
                                done = (WIDES + 2) * (n - 1) + 2 + w
                                dve.wait_ge(g_v, done)
                                nc.vector.tensor_scalar(hot_w, iota_w, rel_w[0], None, ALU.is_equal).then_inc(g_hot, 1)
                                dve.wait_ge(g_hot, WIDES * (n - 1) + w + 1)
                                nc.vector.tensor_scalar(rel_w[0], rel_w[0], -float(WIDE), None, ALU.add).then_inc(g_v, 1)
                                dve.wait_ge(g_sum, WIDES * (n - 1) + w + 1)
                                to = sums[:, 0, ds(w * WIDE, WIDE)]
                                nc.vector.tensor_tensor(to, to, zp[1][:, 0:WIDE], ALU.add)
                                to = sums[:, 1, ds(w * WIDE, WIDE)]
                                nc.vector.tensor_tensor(to, to, zp[1][:, WIDE:2 * WIDE], ALU.add)
                            nc.vector.tensor_copy(rel_w[1], rel_w[0]).then_inc(g_start, 1)

                branches(dve, general, windowed)

            @block.tensor
            def _(pe):
                def bias(to, width):
                    nc.tensor.matmul(to, ones_bf[:, :], b2_parts.rearrange("p t d -> p (t d)")[:, 0:width],
                                     start=True, stop=True, skip_group_check=True)

                def windowed():
                    def transposes(s, j, first):
                        pe.wait_ge(a_done, s + 1)
                        if not first:
                            pe.wait_ge(aT_done, s)
                        for t in range(HALF):
                            last = nc.tensor.transpose(tp[:, t * P:(t + 1) * P], act_in[j % 2][:, t, :], ident[:, :])
                        last.then_inc(tr_done, 1)

                    def z_products(s, c, j, round_end, first):
                        k, b = j // 2, j % 2
                        if b == 0:
                            pe.wait_ge(lhs_in[k], 32 * round_end)
                            pe.wait_ge(hotT_done, c + 1)
                        if not first:
                            pe.wait_ge(z_sum, s - 1)
                        for t in range(HALF):
                            e0 = (b * HALF + t) * P
                            last = nc.tensor.matmul(zp[b][:, t * 2 * D:(t + 1) * 2 * D], lhs[k][:, e0:e0 + P],
                                                    rhs[k][:, :], start=(t % 2 == 0), stop=True, skip_group_check=True)
                        last.then_inc(z_done, 1)

                    def w2_products(s, j, first):
                        b = j % 2
                        pe.wait_ge(aT_done, s + 1)
                        if not first:
                            pe.wait_ge(msg_done, s - 1)
                        bias(mp[b][:, :], HALF * D)
                        for t in range(HALF):
                            last = nc.tensor.matmul(mp[b][:, t * D:(t + 1) * D], act_T[b][:, t * P:(t + 1) * P],
                                                    w2_sb[:, :], start=False, stop=True, skip_group_check=True)
                        last.then_inc(w2_done, 1)

                    def add_messages(s, c, j, first):
                        k, b = j // 2, j % 2
                        pe.wait_ge(msg_done, s + 1)
                        if b == 0:
                            pe.wait_ge(hot_done, c + 1)
                            pe.wait_ge(hot_bf_done, c + 1)
                            if not first:
                                pe.wait_ge(sums_done, c)
                        for t in range(HALF):
                            nc.tensor.matmul(sp_[:, 0:WINDOW], msg[b][:, t, :], hot[k][:, b * HALF + t, :],
                                             start=(b == 0 and t == 0), stop=True, skip_group_check=True)
                        for t in range(HALF):
                            last = nc.tensor.matmul(sp_[:, WINDOW:2 * WINDOW], ones_bf[:, :],
                                                    hot_bf[k][:, b * HALF + t, :],
                                                    start=False, stop=True, skip_group_check=True)
                        last.then_inc(added, 1)

                    def steps(i, first):
                        for j in range(4):
                            s, c = 4 * i + j, 2 * i + j // 2
                            if not (first and j == 0):
                                transposes(s - 1, (j - 1) % 4, first and j == 1)
                            z_products(s, c, j, i + 1, first and j < 2)
                            if not (first and j == 0):
                                w2_products(s - 1, (j - 1) % 4, first and j <= 2)
                            if not (first and j < 2):
                                add_messages(s - 2, c - 1, (j - 2) % 4, first and j < 4)

                    steps(0, True)
                    with pe.Fori(1, ROUNDS) as i:
                        steps(i, False)
                    s = 4 * ROUNDS
                    transposes(s - 1, 3, False)
                    w2_products(s - 1, 3, False)
                    add_messages(s - 2, CHUNKS - 1, 2, False)
                    add_messages(s - 1, CHUNKS - 1, 3, False)

                def general():
                    with pe.Fori(0, CHUNKS) as c:
                        pe.wait_ge(g_in, 48 * (c + 1))
                        for t in range(TILES):
                            n = TILES * c + t + 1
                            pe.wait_ge(g_start, n)
                            nc.tensor.matmul(zp[0][:, 0:2 * D], lhs[0][0:ED, t * P:(t + 1) * P], rhs[0][0:ED, :],
                                             start=True, stop=True).then_inc(g_z, 1)
                            pe.wait_ge(g_a, n)
                            nc.tensor.transpose(tp[:, 0:P], act_in[0][:, 0, :], ident[:, :]).then_inc(g_t, 1)
                            pe.wait_ge(g_aT, n)
                            bias(mp[0][:, 0:D], D)
                            nc.tensor.matmul(mp[0][:, 0:D], act_T[0][:, 0:P], w2_sb[:, :], start=False, stop=True,
                                             skip_group_check=True) \
                                .then_inc(g_w2, 1)
                            pe.wait_ge(g_msg, n)
                            pe.sem_inc(g_windows, 1)
                            with pe.Fori(0, WIDES) as w:
                                pe.wait_ge(g_hot, WIDES * (n - 1) + w + 1)
                                nc.tensor.matmul(zp[1][:, 0:WIDE], msg[0][:, 0, :], hot_w, start=True, stop=True)
                                nc.tensor.matmul(zp[1][:, WIDE:2 * WIDE], ones[:, :], hot_w, start=True, stop=True) \
                                    .then_inc(g_sum, 1)

                branches(pe, general, windowed)

        degree_done = sem("degree_done")
        share_done = sem("share_done")
        mean_done = sem("mean_done")
        silu_done = sem("silu_done")
        up_done = sem("up_done")
        biased = sem("biased")
        gated = sem("gated")
        final_done = sem("final_done")
        out_stored = [sem(f"out_stored{k}") for k in range(4)]
        QUADS = -(-NTILES // 4)
        u_in = [z[k].rearrange("p t c -> p (t c)")[:, 0:512] for k in range(2)]
        u_sig = [sig[k].rearrange("p t c -> p (t c)")[:, 0:512] for k in range(2)]
        u_out = [gath[k // 4].rearrange("p t c -> p (t c)")[:, (k % 4) * 512:(k % 4 + 1) * 512] for k in range(4)]
        up = [mp[0], mp[1]]

        with nc.Block() as block:

            @block.vector
            def _(dve):
                part = NPAD // 4
                for q in range(4):
                    s = slice(q * part, (q + 1) * part)
                    nc.vector.tensor_scalar(sums[:, 1, s], sums[:, 1, s], 1.0, None, ALU.max).then_inc(degree_done, 1)
                    dve.wait_ge(degree_done, q + 1)
                    nc.vector.reciprocal(sums[:, 1, s], sums[:, 1, s]).then_inc(share_done, 1)
                    dve.wait_ge(share_done, q + 1)
                    nc.vector.tensor_tensor(sums[:, 0, s], sums[:, 0, s], sums[:, 1, s], ALU.mult) \
                        .then_inc(mean_done, 1)
                for q in range(QUADS):
                    b, tiles = q % 2, min(4, NTILES - 4 * q)
                    w = tiles * D
                    dve.wait_ge(up_done, q + 1)
                    if q >= 2:
                        dve.wait_ge(final_done, q - 1)
                        dve.wait_ge(gated, q - 1)
                    nc.vector.tensor_tensor(u_in[b][:, 0:w].rearrange("p (t d) -> p t d", d=D),
                                            up[b][:, 0:w].rearrange("p (t d) -> p t d", d=D),
                                            bias_up[:, :].unsqueeze(1).to_broadcast([P, tiles, D]),
                                            ALU.add).then_inc(biased, 1)
                    dve.wait_ge(gated, q + 1)
                    if q >= 4:
                        dve.wait_ge(out_stored[q % 4], 16 * (q // 4))
                    nc.vector.tensor_tensor(u_sig[b][:, 0:w], u_in[b][:, 0:w], u_sig[b][:, 0:w], ALU.mult) \
                        .then_inc(silu_done, 1)
                    dve.wait_ge(silu_done, q + 1)
                    nc.vector.tensor_tensor(u_out[q % 4][:, 0:w], u_sig[b][:, 0:w],
                                            xs[:, 4 * q:4 * q + tiles, :].rearrange("p t d -> p (t d)"),
                                            ALU.add).then_inc(final_done, 1)

            @block.scalar
            def _(act):
                for q in range(QUADS):
                    b, w = q % 2, min(4, NTILES - 4 * q) * D
                    act.wait_ge(biased, q + 1)
                    if q >= 2:
                        act.wait_ge(final_done, q - 1)
                    nc.scalar.activation(u_sig[b][:, 0:w], u_in[b][:, 0:w], ACT.Sigmoid).then_inc(gated, 1)

            @block.tensor
            def _(pe):
                for q in range(QUADS):
                    b, tiles = q % 2, min(4, NTILES - 4 * q)
                    if q >= 2:
                        pe.wait_ge(biased, q - 1)
                    for t in range(4 * q, 4 * q + tiles):
                        n0 = node_start(t)
                        pe.wait_ge(mean_done, min(4, (n0 + P - 1) // (NPAD // 4) + 1))
                        o = up[b][:, (t % 4) * D:(t % 4 + 1) * D]
                        nc.tensor.matmul(o, hT[:, t, :], wu_sb[:, 0, :], start=True, stop=True, skip_group_check=True)
                        last = nc.tensor.matmul(o, sums[:, 0, n0:n0 + P], wu_sb[:, 1, :], start=False, stop=True,
                                                skip_group_check=True)
                    last.then_inc(up_done, 1)

            @block.sync
            def _(sp):
                for q in range(QUADS):
                    tiles = min(4, NTILES - 4 * q)
                    sp.wait_ge(final_done, q + 1)
                    if tiles == 4:
                        sp.dma_start(out[4 * q * P:4 * (q + 1) * P, :].rearrange("(t p) d -> p t d", p=P),
                                     u_out[q % 4][:, :].rearrange("p (t d) -> p t d", d=D)).then_inc(out_stored[q % 4], 16)
                    else:
                        sp.dma_start(out[N - P + NODE_REPEATED:N, :], u_out[q % 4][NODE_REPEATED:P, 0:D]) \
                            .then_inc(out_stored[q % 4], 16)
                for k in range(4):
                    sp.wait_ge(out_stored[k], 16 * len(range(k, QUADS, 4)))


def kernel(**inputs):
    import numpy as np
    import concourse.bacc as bacc
    from concourse.bass_utils import run_bass_kernel_spmd as run

    edge = np.concatenate([np.arange((CHUNKS - 1) * CHUNK), np.arange(E - CHUNK, E)])
    src = np.asarray(inputs["src"])[edge].reshape(CHUNKS, TILES, P)
    dst = np.asarray(inputs["dst"])[edge].reshape(CHUNKS, TILES, P)
    e = np.asarray(inputs["edge_attr_64"])[edge].reshape(CHUNKS, CHUNK, ED)
    arrays = {
        "x": inputs["x"],
        "src_ch": src.transpose(0, 2, 1),
        "dst_rows": dst.reshape(CHUNKS, CHUNK),
        "dst_cols": dst.transpose(2, 0, 1).reshape(P, CHUNKS * TILES),
        "dst_first": dst[:, 0, 0].reshape(1, CHUNKS),
        "e_ch": e.transpose(0, 2, 1),
        **{k: inputs["L0_gnn_" + k] for k in ("w1", "b1", "w2", "b2", "wg", "bg", "wu", "bu")},
    }
    nc = bacc.Bacc("TRN2", target_bir_lowering=False, num_devices=1)
    args, maps = [], {}
    for name, a in arrays.items():
        a = np.ascontiguousarray(a)
        maps[f"in_{name}"] = a
        args.append(nc.dram_tensor(f"in_{name}", a.shape, mybir.dt.from_np(a.dtype), kind="ExternalInput").ap())
    args.append(nc.dram_tensor("out", (N, D), mybir.dt.float32, kind="ExternalOutput").ap())
    gnn_program(nc, *args)
    return run(nc, [maps], core_ids=[0]).results[0]["out"]
```

```python
import concourse.bass as bass
from concourse import mybir
from contextlib import ExitStack

N, E, D, ED = 6250, 200000, 128, 64
P = 128
TILES = 8
HALF = TILES // 2
CHUNK = TILES * P
CHUNKS = -(-E // CHUNK)
REPEATED = CHUNKS * CHUNK - E
ROUNDS = CHUNKS // 2
WINDOW = 64
LAST_BASE = N - WINDOW
NTILES = -(-N // P)
NODE_REPEATED = NTILES * P - N
WIDE = 512
WIDES = -(-N // WIDE)
NPAD = WIDES * WIDE
FOREIGN = -1.0e6
EPS = 1e-5
QUAD = 4
QUADS = -(-NTILES // QUAD)
STATS = [0, 8, 20, 32, NTILES]
assert CHUNKS % 2 == 0


def node_start(t):
    return min(t * P, N - P)


def quad_tiles(q):
    return range(QUAD * q, min(QUAD * (q + 1), NTILES))


def gnn_program(nc, x, src_ch, dst_rows, dst_cols, dst_first, e_ch, w_z, w_sq, biases, out):
    fp32, bf16, i32 = mybir.dt.float32, mybir.dt.bfloat16, mybir.dt.int32
    ALU = mybir.AluOpType
    ACT = mybir.ActivationFunctionType
    AX = mybir.AxisListType.X
    ds = bass.ds

    src_table = nc.dram_tensor("src_table", [N, 2 * D], fp32, kind="Internal").ap()
    dst_table = nc.dram_tensor("dst_table", [N, 2 * D], fp32, kind="Internal").ap()
    src_rows2 = src_ch.rearrange("c p t -> (c p) t")
    e_rows = e_ch.rearrange("c f n -> (c f) n")

    ctx = ExitStack()
    with ctx:
        def sb(name, shape, dt=fp32):
            return ctx.enter_context(nc.sbuf_tensor(name, shape, dt))

        def pb(name, shape):
            return ctx.enter_context(nc.psum_tensor(name, shape, fp32))

        def sem(name):
            return ctx.enter_context(nc.semaphore(name))

        xs = sb("xs", [P, NTILES, D])
        hT = sb("hT", [P, NTILES, P])
        sums = sb("sums", [P, 2, NPAD])
        own = hT
        bn = sb("bn", [P, NTILES, 6])
        stat = sb("stat", [P, 4, NTILES])
        degree = sb("degree", [P, NTILES])
        w_node = sb("w_node", [P, 4 * D])
        w_square = sb("w_square", [P, 3, D])
        w2_sb, wu_h, wu_mean = (w_square[:, k, :] for k in range(3))
        b_all = sb("b_all", [P, 4, D])
        b_rest = sb("b_rest", [P, 2, D])
        b_parts = sb("b_parts", [P, 2, QUAD, D], bf16)
        ident = sb("ident", [P, P])
        ones_bf = sb("ones_bf", [P, P], bf16)
        ones = sb("ones", [P, P])
        iota_i = sb("iota_i", [P, WIDE], i32)
        iota_f = sb("iota_f", [P, WIDE])
        row_i = sb("row_i", [P, 1], i32)
        row_f = sb("row_f", [P, 1])
        dcol_i = sb("dcol_i", [P, CHUNKS * TILES], i32)
        dcol = sb("dcol", [P, CHUNKS * TILES])
        drel = sb("drel", [P, CHUNKS * TILES])
        first_i = sb("first_i", [P, CHUNKS], i32)
        base_i = sb("base_i", [P, CHUNKS], i32)
        base_f = sb("base_f", [P, CHUNKS])
        own_node = sb("own_node", [P, CHUNKS])
        outside = sb("outside", [P, 2])
        flag_i = sb("flag_i", [1, 1], i32)
        lhs = [sb(f"lhs{k}", [P, CHUNK]) for k in range(2)]
        rhs = [sb(f"rhs{k}", [P, 2 * D]) for k in range(2)]
        dst_row = [sb(f"dst_row{k}", [P, CHUNK], i32) for k in range(2)]
        idx = [sb(f"idx{k}", [P, TILES], i32) for k in range(2)]
        gath = [sb(f"gath{k}", [P, TILES, 2 * D]) for k in range(2)]
        z = [sb(f"z{k}", [P, HALF, 2 * D]) for k in range(2)]
        sig = [sb(f"sig{k}", [P, HALF, 2 * D]) for k in range(2)]
        act_in = [sb(f"a{k}", [P, HALF, D]) for k in range(2)]
        act_T = [sb(f"aT{k}", [P, HALF * P]) for k in range(2)]
        msg = [sb(f"msg{k}", [P, HALF, D]) for k in range(2)]
        hot = [sb(f"hot{k}", [P, TILES, WINDOW]) for k in range(2)]
        count = [sb(f"count{k}", [P, WINDOW], bf16) for k in range(2)]
        flat = lambda a: a[:, :, :].rearrange("p t c -> p (t c)")
        normed = [act_in[0], act_in[1], msg[0], msg[1]]
        stage_src = [flat(gath[k // 2])[:, (k % 2) * 1024:(k % 2 + 1) * 1024] for k in range(4)]
        stage_dst = [flat(z[0]), flat(z[1]), flat(sig[0]), flat(sig[1])]

        zp = [pb(f"zp{k}", [P, HALF * 2 * D]) for k in range(2)]
        tp = pb("tp", [P, 512])
        mp = [pb(f"mp{k}", [P, 512]) for k in range(2)]
        sp_ = pb("sum_p", [P, 512])

        x_in = [sem(f"x_in{g}") for g in range(len(STATS) - 1)]
        w_in = sem("w_in")
        edge_w_in = sem("edge_w_in")
        d_in = sem("d_in")
        pool_chain = sem("pool_chain")
        made = sem("made")
        prepared = sem("prepared")
        zeroed = sem("zeroed")
        dve_chain = sem("dve_chain")
        b2_done = sem("b2_done")
        var_done = sem("var_done")
        dev_done = sem("dev_done")
        normed_done = sem("normed_done")
        h_tr = sem("h_tr")
        hT_done = sem("hT_done")
        tab_src = sem("tab_src")
        tab_dst = sem("tab_dst")
        own_up = sem("own_up")
        own_done = sem("own_done")
        staged_src = sem("staged_src")
        staged_dst = sem("staged_dst")
        src_stored = [sem(f"src_stored{k}") for k in range(4)]
        dst_stored = [sem(f"dst_stored{k}") for k in range(4)]
        windows_checked = sem("windows_checked")
        outside_sum = sem("outside_sum")
        flag_done = sem("flag_done")

        def all_stored(eng, stored):
            for k in range(4):
                eng.wait_ge(stored[k], 16 * len(range(k, QUADS, 4)))

        def load_x(sp):
            for g in range(len(STATS) - 1):
                for t0 in range(STATS[g], min(STATS[g + 1], N // P), QUAD):
                    sp.dma_start(xs[:, t0:t0 + QUAD, :], x[t0 * P:(t0 + QUAD) * P, :].rearrange("(t p) d -> p t d", p=P)) \
                        .then_inc(x_in[g], 16)
            sp.dma_start(xs[:, NTILES - 1, :], x[N - P:N, :]).then_inc(x_in[-1], 16)

        def store_tables(sp):
            for table, staged, stage, stored in ((src_table, staged_src, stage_src, src_stored),
                                                 (dst_table, staged_dst, stage_dst, dst_stored)):
                for q in range(QUADS):
                    sp.wait_ge(staged, q + 1)
                    if len(quad_tiles(q)) == QUAD:
                        n0 = q * QUAD * P
                        sp.dma_start(table[n0:n0 + QUAD * P, :].rearrange("(t p) c -> p t c", p=P),
                                     stage[q % 4].rearrange("p (t c) -> p t c", t=QUAD)).then_inc(stored[q % 4], 16)
                    else:
                        sp.dma_start(table[N - P + NODE_REPEATED:N, :], stage[q % 4][NODE_REPEATED:P, 0:2 * D]) \
                            .then_inc(stored[q % 4], 16)

        def prepare(pool):
            links = [0]

            def link(ins):
                links[0] += 1
                ins.then_inc(pool_chain, 1)
                pool.wait_ge(pool_chain, links[0])

            link(pool.memset(ident[:, :], 0.0))
            pool.affine_select(out=ident[:, :], in_=ident[:, :], compare_op=ALU.not_equal, fill=1.0,
                               base=0, pattern=[[-1, P]], channel_multiplier=1).then_inc(made, 1)
            pool.memset(ones_bf[:, :], 1.0).then_inc(made, 1)
            pool.memset(ones[:, :], 1.0).then_inc(made, 1)
            pool.iota(iota_i[:, :], pattern=[[1, WIDE]], base=0, channel_multiplier=0).then_inc(pool_chain, 1)
            pool.iota(row_i[:, :], pattern=[[0, 1]], base=-WINDOW, channel_multiplier=1).then_inc(pool_chain, 1)
            links[0] += 2
            pool.wait_ge(pool_chain, links[0])
            pool.tensor_copy(iota_f[:, :], iota_i[:, :]).then_inc(prepared, 1)
            link(pool.tensor_copy(row_f[:, :], row_i[:, :]))
            pool.wait_ge(d_in, 32)
            link(pool.tensor_scalar(base_f[:, :], first_i[:, :], float(LAST_BASE), None, ALU.min))
            pool.tensor_copy(base_i[:, :], base_f[:, :]).then_inc(prepared, 1)
            pool.tensor_scalar(own_node[:, :], base_f[:, :], row_f[:, 0:1], None, ALU.add).then_inc(prepared, 1)
            link(pool.tensor_copy(dcol[:, :], dcol_i[:, :]))
            link(pool.tensor_tensor(drel[:, :].rearrange("p (c t) -> p c t", t=TILES),
                                    dcol[:, :].rearrange("p (c t) -> p c t", t=TILES),
                                    base_f[:, :].unsqueeze(2).to_broadcast([P, CHUNKS, TILES]), ALU.subtract))
            pool.sem_inc(prepared, 1)
            pool.memset(sums[:, 0, :], 0.0).then_inc(zeroed, 1)
            pool.memset(sums[:, 1, :], 0.0).then_inc(zeroed, 1)

        def check_windows(dve):
            dve.wait_ge(prepared, 4)
            dve_link(dve, nc.vector.tensor_reduce(outside[:, 0:1], drel[:, :], AX, ALU.min))
            dve_link(dve, nc.vector.tensor_reduce(outside[:, 1:2], drel[:, :], AX, ALU.max))
            dve_link(dve, nc.vector.tensor_scalar(outside[:, 0:1], outside[:, 0:1], 0.0, None, ALU.is_lt))
            dve_link(dve, nc.vector.tensor_scalar(outside[:, 1:2], outside[:, 1:2], float(WINDOW - 1), None, ALU.is_gt))
            c0 = (CHUNKS - 1) * TILES
            full, rest = REPEATED // P, REPEATED % P
            for m in (drel, dcol):
                dve_link(dve, nc.vector.memset(m[:, c0:c0 + full], FOREIGN))
                if rest:
                    dve_link(dve, nc.vector.memset(m[0:rest, c0 + full:c0 + full + 1], FOREIGN))
            dve.sem_inc(windows_checked, 1)

        dve_links = [0]

        def dve_link(dve, ins):
            dve_links[0] += 1
            ins.then_inc(dve_chain, 1)
            dve.wait_ge(dve_chain, dve_links[0])

        def load_weights(act):
            act.dma_start(w_node[:, :].rearrange("p (k c) -> p k c", k=2), w_z[0:2 * D, :].rearrange("(k p) c -> p k c", p=P)) \
                .then_inc(w_in, 16)
            act.dma_start(first_i[:, :], dst_first[:, :].to_broadcast([P, CHUNKS])).then_inc(d_in, 16)
            act.dma_start(dcol_i[:, :], dst_cols[:, :]).then_inc(d_in, 16)
            act.dma_start(b_all[:, :, :].rearrange("p k d -> p (k d)"), biases[:, :].to_broadcast([P, 4 * D])) \
                .then_inc(edge_w_in, 16)
            act.dma_start(w_square[:, :, :], w_sq.rearrange("(k p) d -> p k d", p=P)).then_inc(edge_w_in, 16)
            for to in rhs:
                act.dma_start(to[0:ED, :], w_z[2 * D:2 * D + ED, :]).then_inc(edge_w_in, 16)

        W_NODE, W_EDGE = 16, 16 * 4

        def nodes_act(act):
            def deviation(g):
                act.wait_ge(var_done, g + 1)
                s = slice(STATS[g], STATS[g + 1])
                nc.scalar.activation(stat[:, 2, s], stat[:, 1, s], ACT.Sqrt).then_inc(dev_done, 1)

            def src_rows(q):
                w = len(quad_tiles(q)) * 2 * D
                act.wait_ge(tab_src, q + 1)
                if q >= 4:
                    act.wait_ge(src_stored[q % 4], 16 * (q // 4))
                nc.scalar.copy(stage_src[q % 4][:, 0:w], zp[q % 2][:, 0:w]).then_inc(staged_src, 1)

            deviation(0)
            for q in range(QUADS):
                w = len(quad_tiles(q)) * P
                act.wait_ge(h_tr, q + 1)
                nc.scalar.activation(hT[:, QUAD * q:QUAD * q + w // P, :].rearrange("p t n -> p (t n)"), mp[q % 2][:, 0:w],
                                     ACT.Relu).then_inc(hT_done, 1)
                if q >= 1:
                    src_rows(q - 1)
                if QUAD * (q + 1) in STATS[1:-1]:
                    deviation(STATS.index(QUAD * (q + 1)))
            src_rows(QUADS - 1)
            for q in range(QUADS):
                w = len(quad_tiles(q)) * D
                act.wait_ge(own_up, q + 1)
                nc.scalar.copy(own[:, QUAD * q:QUAD * q + w // D, :].rearrange("p t d -> p (t d)"), mp[q % 2][:, 0:w]) \
                    .then_inc(own_done, 1)

        def nodes_dve(dve):
            def statistics(g):
                a, b = STATS[g], STATS[g + 1]
                dve.wait_ge(x_in[g], 16 * -(-(b - a) // QUAD))
                for t in range(a, b):
                    last = nc.vector.bn_stats(bn[:, t, :], xs[:, t, :])
                dve_link(dve, last)
                even, odd, half = bn[:, a:b, 1], bn[:, a:b, 4], 0.5
                mean, var, scr = stat[:, 0, a:b], stat[:, 1, a:b], stat[:, 3, a:b]
                dve_link(dve, nc.vector.tensor_tensor(scr, even, odd, ALU.subtract))
                dve_link(dve, nc.vector.tensor_tensor(mean, even, odd, ALU.add))
                dve_link(dve, nc.vector.tensor_scalar(mean, mean, half, None, ALU.mult))
                dve_link(dve, nc.vector.tensor_tensor(scr, scr, scr, ALU.mult))
                dve_link(dve, nc.vector.tensor_scalar(scr, scr, half * half, EPS, ALU.mult, ALU.add))
                dve_link(dve, nc.vector.tensor_tensor(var, bn[:, a:b, 2], bn[:, a:b, 5], ALU.add))
                dve_link(dve, nc.vector.tensor_scalar(var, var, 1.0 / D, None, ALU.mult))
                nc.vector.tensor_tensor(var, var, scr, ALU.add).then_inc(var_done, 1)

            def normalise(g):
                a, b = STATS[g], STATS[g + 1]
                dve.wait_ge(dev_done, g + 1)
                dve_link(dve, nc.vector.reciprocal(stat[:, 2, a:b], stat[:, 2, a:b]))
                for q in range(a // QUAD, -(-b // QUAD)):
                    if q >= 4:
                        dve.wait_ge(h_tr, q - 3)
                    for t in quad_tiles(q):
                        last = nc.vector.tensor_scalar(normed[q % 4][:, t % QUAD, :], xs[:, t, :], stat[:, 0, t:t + 1],
                                                       stat[:, 2, t:t + 1], ALU.subtract, ALU.mult)
                    last.then_inc(normed_done, 1)

            for g in range(len(STATS) - 1):
                statistics(g)
                normalise(g)
            check_windows(dve)
            dve.wait_ge(edge_w_in, W_EDGE)
            dve_link(dve, nc.vector.memset(b_parts[:, :, :, :], 0.0))
            for row in (0, 32, 64):
                at = slice(row, row + 1)
                whole, rest = b_all[at, 2:4, :], b_rest[at, :, :]
                part = b_parts[at, :, 0, :]
                dve_link(dve, nc.vector.tensor_copy(part, whole))
                if row >= 32:
                    dve_link(dve, nc.vector.tensor_tensor(rest, whole, part, ALU.subtract))
                    dve_link(dve, nc.vector.tensor_copy(part, rest))
                if row == 64:
                    dve_link(dve, nc.vector.tensor_tensor(whole, rest, part, ALU.subtract))
                    dve_link(dve, nc.vector.tensor_copy(part, whole))
            for j in range(1, QUAD):
                ins = nc.vector.tensor_copy(b_parts[:, :, j, :], b_parts[:, :, 0, :])
                ins.then_inc(b2_done, 1)
            for q in range(QUADS):
                tiles = len(quad_tiles(q))
                dve.wait_ge(tab_dst, q + 1)
                if q >= 4:
                    dve.wait_ge(dst_stored[q % 4], 16 * (q // 4))
                nc.vector.tensor_tensor(stage_dst[q % 4][:, 0:tiles * 2 * D].rearrange("p (t c) -> p t c", t=tiles),
                                        zp[(QUADS + q) % 2][:, 0:tiles * 2 * D].rearrange("p (t c) -> p t c", t=tiles),
                                        b_all[:, 0:2, :].rearrange("p k d -> p (k d)").unsqueeze(1)
                                        .to_broadcast([P, tiles, 2 * D]),
                                        ALU.add).then_inc(staged_dst, 1)
                if q == 0:
                    dve.wait_ge(outside_sum, 1)
                    nc.vector.tensor_copy(flag_i[:, :], tp[0:1, 0:1]).then_inc(flag_done, 1)

        def bias(to, which, width):
            nc.tensor.matmul(to, ones_bf[:, :], b_parts[:, which, 0:width // D, :].rearrange("p t d -> p (t d)"),
                             start=True, stop=True, skip_group_check=True)

        def nodes_pe(pe):
            def products(q, bank, half, done):
                for t in quad_tiles(q):
                    last = nc.tensor.matmul(zp[bank][:, (t % QUAD) * 2 * D:(t % QUAD + 1) * 2 * D], hT[:, t, :],
                                            w_node[:, half * 2 * D:(half + 1) * 2 * D], start=(t % 2 == 0), stop=True,
                                            skip_group_check=True)
                last.then_inc(done, 1)

            def src_products(q):
                pe.wait_ge(hT_done, q + 1)
                if q >= 2:
                    pe.wait_ge(staged_src, q - 1)
                products(q, q % 2, 0, tab_src)

            pe.wait_ge(made, 3)
            pe.wait_ge(w_in, W_NODE)
            for q in range(QUADS):
                pe.wait_ge(normed_done, q + 1)
                if q >= 2:
                    pe.wait_ge(hT_done, q - 1)
                for t in quad_tiles(q):
                    last = nc.tensor.transpose(mp[q % 2][:, (t % QUAD) * P:(t % QUAD + 1) * P],
                                               normed[q % 4][:, t % QUAD, :], ident[:, :])
                last.then_inc(h_tr, 1)
                if q >= 1:
                    src_products(q - 1)
            src_products(QUADS - 1)
            pe.wait_ge(windows_checked, 1)
            nc.tensor.matmul(tp[0:1, 0:1], outside[:, 0:1], ones[:, 0:1], start=True, stop=False)
            nc.tensor.matmul(tp[0:1, 0:1], outside[:, 1:2], ones[:, 0:1], start=False, stop=True) \
                .then_inc(outside_sum, 1)
            for q in range(QUADS):
                bank = (QUADS + q) % 2
                if q < 2:
                    pe.wait_ge(staged_src, QUADS - 1 + q)
                else:
                    pe.wait_ge(staged_dst, q - 1)
                products(q, bank, 1, tab_dst)
            pe.wait_ge(b2_done, QUAD - 1)
            pe.wait_ge(edge_w_in, W_EDGE)
            for q in range(QUADS):
                w = len(quad_tiles(q)) * D
                if q >= 2:
                    pe.wait_ge(own_done, q - 1)
                bias(mp[q % 2][:, 0:w], 1, w)
                for t in quad_tiles(q):
                    last = nc.tensor.matmul(mp[q % 2][:, (t % QUAD) * D:(t % QUAD + 1) * D], hT[:, t, :], wu_h,
                                            start=False, stop=True, skip_group_check=True)
                last.then_inc(own_up, 1)

        lhs_in = [sem(f"lhs_in{k}") for k in range(2)]
        dst_in = [sem(f"dst_in{k}") for k in range(2)]
        idx_in = [sem(f"idx_in{k}") for k in range(2)]
        gathered = [sem(f"gathered{j}") for j in range(4)]
        opened = sem("opened")
        hotT_done = sem("hotT_done")
        hot_done = sem("hot_done")
        count_done = sem("count_done")
        z_done = sem("z_done")
        z_sum = sem("z_sum")
        sig_done = sem("sig_done")
        a_done = sem("a_done")
        tr_done = sem("tr_done")
        aT_done = sem("aT_done")
        w2_done = sem("w2_done")
        msg_done = sem("msg_done")
        added = sem("added")
        sums_done = sem("sums_done")

        edges_done = sem("edges_done")

        g_start = sem("g_start")
        g_in = sem("g_in")
        g_rows = sem("g_rows")
        g_z = sem("g_z")
        g_zs = sem("g_zs")
        g_sig = sem("g_sig")
        g_a = sem("g_a")
        g_t = sem("g_t")
        g_aT = sem("g_aT")
        g_w2 = sem("g_w2")
        g_msg = sem("g_msg")
        g_hot = sem("g_hot")
        g_sum = sem("g_sum")
        g_v = sem("g_v")
        g_added = sem("g_added")
        g_windows = sem("g_windows")
        gdst = dst_row[0][:, 0:TILES]
        iota_w = iota_f[:, :]
        hot_w = hot[1].rearrange("p t n -> p (t n)")[:, 0:WIDE]
        rel_w = outside[:, 0:1]

        def branches(eng, general, windowed):
            eng.wait_ge(flag_done, 1)
            general_case = eng.value_load(flag_i[0:1, 0:1], min_val=0, max_val=2 * P)
            with eng.If(general_case > 0):
                general()
            with eng.Else():
                windowed()
            eng.nop()

        SPARE = 8
        degree_T = sem("degree_T")
        degree_up = sem("degree_up")
        share_done = sem("share_done")
        up_done = sem("up_done")
        scaled = sem("scaled")
        up_sum = sem("up_sum")
        silu_done = sem("silu_done")
        final_done = sem("final_done")
        out_stored = [sem(f"out_stored{k}") for k in range(4)]
        u_in = [flat(z[k])[:, 0:QUAD * D] for k in range(2)]
        u_scaled = [flat(z[k])[:, QUAD * D:2 * QUAD * D] for k in range(2)]
        u_silu = [flat(sig[k])[:, 0:QUAD * D] for k in range(2)]
        u_out = [flat(gath[0])[:, k * QUAD * D:(k + 1) * QUAD * D] for k in range(4)]

        def update_pe(pe):
            pe.wait_ge(edges_done, 1)
            for t in range(NTILES):
                n0 = node_start(t)
                last = nc.tensor.transpose(tp[:, t * SPARE:(t + 1) * SPARE], sums[0:SPARE, 1, n0:n0 + P],
                                           ident[0:SPARE, 0:SPARE])
            last.then_inc(degree_T, 1)
            for q in range(QUADS):
                if q >= 2:
                    pe.wait_ge(scaled, q - 1)
                for t in quad_tiles(q):
                    n0, o = node_start(t), (t % QUAD) * D
                    last = nc.tensor.matmul(zp[q % 2][:, o:o + D], sums[:, 0, n0:n0 + P], wu_mean, start=True, stop=True,
                                            skip_group_check=True)
                last.then_inc(up_done, 1)

        def update_dve(dve):
            dve.wait_ge(degree_T, 1)
            nc.vector.tensor_scalar(degree[:, :],
                                    tp[:, 0:NTILES * SPARE].rearrange("p (t k) -> p t k", k=SPARE)[:, :, 0], 1.0, None, ALU.max).then_inc(degree_up, 1)
            dve.wait_ge(degree_up, 1)
            nc.vector.reciprocal(degree[:, :], degree[:, :]).then_inc(share_done, 1)
            dve.wait_ge(share_done, 1)
            for q in range(QUADS):
                b, tiles = q % 2, len(quad_tiles(q))
                w = tiles * D
                dve.wait_ge(up_done, q + 1)
                if q >= 2:
                    dve.wait_ge(silu_done, q - 1)
                nc.vector.tensor_tensor(u_scaled[b][:, 0:w].rearrange("p (t d) -> p t d", t=tiles),
                                        zp[b][:, 0:w].rearrange("p (t d) -> p t d", t=tiles),
                                        degree[:, QUAD * q:QUAD * q + tiles].unsqueeze(2).to_broadcast([P, tiles, D]),
                                        ALU.mult).then_inc(scaled, 1)
                dve.wait_ge(scaled, q + 1)
                nc.vector.tensor_tensor(u_in[b][:, 0:w], u_scaled[b][:, 0:w], own[:, QUAD * q:QUAD * q + tiles, :].rearrange("p t d -> p (t d)"), ALU.add) \
                    .then_inc(up_sum, 1)

        def update_act(act):
            for q in range(QUADS):
                b, w = q % 2, len(quad_tiles(q)) * D
                act.wait_ge(up_sum, q + 1)
                if q >= 2:
                    act.wait_ge(final_done, q - 1)
                nc.scalar.activation(u_silu[b][:, 0:w], u_in[b][:, 0:w], ACT.Silu).then_inc(silu_done, 1)

        def update_pool(pool):
            for q in range(QUADS):
                tiles = len(quad_tiles(q))
                w = tiles * D
                pool.wait_ge(silu_done, q + 1)
                if q >= 4:
                    pool.wait_ge(out_stored[q % 4], 16 * (q // 4))
                pool.tensor_tensor(u_out[q % 4][:, 0:w], u_silu[q % 2][:, 0:w],
                                   xs[:, QUAD * q:QUAD * q + tiles, :].rearrange("p t d -> p (t d)"),
                                   ALU.add).then_inc(final_done, 1)

        def store_out(sp):
            for q in range(QUADS):
                sp.wait_ge(final_done, q + 1)
                if len(quad_tiles(q)) == QUAD:
                    n0 = QUAD * q * P
                    sp.dma_start(out[n0:n0 + QUAD * P, :].rearrange("(t p) d -> p t d", p=P),
                                 u_out[q % 4][:, :].rearrange("p (t d) -> p t d", d=D)).then_inc(out_stored[q % 4], 16)
                else:
                    sp.dma_start(out[N - P + NODE_REPEATED:N, :], u_out[q % 4][NODE_REPEATED:P, 0:D]) \
                        .then_inc(out_stored[q % 4], 16)
            for k in range(4):
                sp.wait_ge(out_stored[k], 16 * len(range(k, QUADS, 4)))

        with nc.Block() as block:

            @block.sync
            def _(sp):
                def load_edges(c, k):
                    sp.dma_start(dst_row[k][WINDOW:P, :], dst_rows[ds(c, 1), :].to_broadcast([WINDOW, CHUNK])) \
                        .then_inc(dst_in[k], 16)
                    sp.dma_start(lhs[k][0:ED, :], e_rows[ds(c * ED, ED), :]).then_inc(lhs_in[k], 16)

                def load_indices(c, k):
                    sp.dma_start(idx[k][:, :], src_rows2[ds(c * P, P), :]).then_inc(idx_in[k], 16)

                def load_window(c, k):
                    base = sp.value_load(base_i[0:1, ds(c, 1)], min_val=0, max_val=LAST_BASE)
                    sp.dma_start(rhs[k][WINDOW:P, :], dst_table[ds(base, WINDOW), :]).then_inc(lhs_in[k], 16)

                def windowed():
                    def load(i, k):
                        c = 2 * i + k
                        for j in (2 * k, 2 * k + 1):
                            sp.wait_ge(gathered[j], 64 * i)
                        load_indices(c, k)
                        sp.wait_ge(z_done, 2 * c - 2)
                        load_edges(c, k)
                        load_window(c, k)

                    for k in range(2):
                        load_window(k, k)
                    with sp.Fori(1, ROUNDS) as i:
                        for k in range(2):
                            load(i, k)

                def general():
                    for k in range(2):
                        sp.wait_ge(idx_in[k], 16)
                        sp.wait_ge(dst_in[k], 16)
                        sp.wait_ge(lhs_in[k], 16)
                    with sp.Fori(0, CHUNKS) as c:
                        sp.wait_ge(g_start, TILES * c + 1)
                        sp.dma_start(idx[0][:, :], src_rows2[ds(c * P, P), :]).then_inc(g_in, 16)
                        sp.dma_start(gdst, dst_cols[:, ds(c * TILES, TILES)]).then_inc(g_in, 16)
                        sp.dma_start(lhs[0][0:ED, :], e_rows[ds(c * ED, ED), :]).then_inc(g_in, 16)

                load_x(sp)
                for k in range(2):
                    load_indices(k, k)
                    load_edges(k, k)
                store_tables(sp)
                all_stored(sp, src_stored)
                all_stored(sp, dst_stored)
                sp.wait_ge(prepared, 4)
                branches(sp, general, windowed)
                store_out(sp)

            @block.gpsimd
            def _(pool):
                def gather(table, to, index):
                    return pool.indirect_dma_start(out=to, out_offset=None, in_=table[:, :],
                                                   in_offset=bass.IndirectOffsetOnAxis(ap=index, axis=0))

                def windowed():
                    def gathers(i, first):
                        for j in range(4):
                            k, h0 = j // 2, (j % 2) * HALF
                            if h0 == 0:
                                pool.wait_ge(idx_in[k], 16 * (i + 1))
                            if not first:
                                pool.wait_ge(z_sum, 4 * i + j - 3)
                            pool.sem_inc(opened, 1)
                            for t in range(h0, h0 + HALF):
                                pool.indirect_dma_start(
                                    out=gath[k][:, t, :], out_offset=None, in_=src_table[:, :],
                                    in_offset=bass.IndirectOffsetOnAxis(ap=idx[k][:, t:t + 1], axis=0)).then_inc(gathered[j], 16)

                    gathers(0, True)
                    with pool.Fori(1, ROUNDS) as i:
                        gathers(i, False)

                def general():
                    pool.sem_inc(g_start, 1)
                    all_stored(pool, dst_stored)
                    with pool.Fori(0, CHUNKS) as c:
                        pool.wait_ge(g_in, 48 * (c + 1))
                        for t in range(TILES):
                            pool.wait_ge(g_start, TILES * c + t + 1)
                            pool.sem_inc(opened, 1)
                            gather(src_table, gath[0][:, 0, :], idx[0][:, t:t + 1]).then_inc(g_rows, 16)
                            gather(dst_table, gath[0][:, 1, :], gdst[:, t:t + 1]).then_inc(g_rows, 16)

                prepare(pool)
                all_stored(pool, src_stored)
                branches(pool, general, windowed)
                update_pool(pool)

            @block.scalar
            def _(act):
                def windowed():
                    def transposed(s, b, first):
                        act.wait_ge(tr_done, s + 1)
                        if not first:
                            act.wait_ge(w2_done, s - 1)
                        nc.scalar.copy(act_T[b][:, :], tp[:, :]).then_inc(aT_done, 1)

                    def sigmoids(s, b, first):
                        act.wait_ge(z_sum, s + 1)
                        if not first:
                            act.wait_ge(msg_done, s - 1)
                            act.wait_ge(a_done, s - 1)
                        nc.scalar.activation(sig[b][:, :, :], z[b][:, :, :], ACT.Sigmoid).then_inc(sig_done, 1)

                    def half(s, c, j, first):
                        b = j % 2
                        if not (first and j == 0):
                            transposed(s - 1, 1 - b, first and j <= 2)
                        sigmoids(s, b, first and j < 2)

                    for j in range(4):
                        half(j, j // 2, j, True)
                    with act.Fori(1, ROUNDS) as i:
                        for j in range(4):
                            half(4 * i + j, 2 * i + j // 2, j, False)
                    transposed(4 * ROUNDS - 1, 1, False)

                def general():
                    with act.Fori(0, CHUNKS) as c:
                        for t in range(TILES):
                            n = TILES * c + t + 1
                            act.wait_ge(g_zs, n)
                            nc.scalar.activation(sig[0][:, 0, :], z[0][:, 0, :], ACT.Sigmoid).then_inc(g_sig, 1)
                            act.wait_ge(g_t, n)
                            nc.scalar.copy(act_T[0][:, 0:P], tp[:, 0:P]).then_inc(g_aT, 1)

                load_weights(act)
                nodes_act(act)
                all_stored(act, dst_stored)
                branches(act, general, windowed)
                update_act(act)

            @block.vector
            def _(dve):
                def windowed():
                    def hot_rows(c, k, round_end, first):
                        dve.wait_ge(dst_in[k], 16 * round_end)
                        if not first:
                            dve.wait_ge(z_done, 2 * c - 2)
                        nc.vector.tensor_scalar(lhs[k][WINDOW:P, :], dst_row[k][WINDOW:P, :],
                                                own_node[WINDOW:P, ds(c, 1)], None, ALU.is_equal) \
                            .then_inc(hotT_done, 1)

                    def hot_cols(c, k, first):
                        if not first:
                            dve.wait_ge(added, 2 * c - 2)
                            dve.wait_ge(count_done, c - 1)
                        nc.vector.tensor_tensor(
                            hot[k][:, :, :], iota_f[:, 0:WINDOW].unsqueeze(1).to_broadcast([P, TILES, WINDOW]),
                            drel[:, ds(c * TILES, TILES)].unsqueeze(2).to_broadcast([P, TILES, WINDOW]),
                            ALU.is_equal).then_inc(hot_done, 1)

                    def hot_sum(c, k, first):
                        dve.wait_ge(hot_done, c + 1)
                        if not first:
                            dve.wait_ge(added, 2 * c - 2)
                        with nc.allow_low_precision("counts up to 8 are exact"):
                            nc.vector.tensor_reduce(count[k][:, :], hot[k][:, :, :].rearrange("p t n -> p n t"), AX,
                                                    ALU.add).then_inc(count_done, 1)

                    def z_add(s, j, round_end, first):
                        b = j % 2
                        dve.wait_ge(z_done, s + 1)
                        dve.wait_ge(gathered[j], 64 * round_end)
                        if not first:
                            dve.wait_ge(sig_done, s - 1)
                            dve.wait_ge(a_done, s - 1)
                        nc.vector.tensor_tensor(
                            z[b][:, :, :], zp[b][:, :].rearrange("p (t c) -> p t c", t=HALF),
                            gath[j // 2][:, b * HALF:(b + 1) * HALF, :], ALU.add).then_inc(z_sum, 1)

                    def a_mul(s, j, first):
                        b = j % 2
                        dve.wait_ge(sig_done, s + 1)
                        if not first:
                            dve.wait_ge(tr_done, s - 1)
                        nc.vector.tensor_tensor(act_in[b][:, :, :], z[b][:, :, 0:D], sig[b][:, :, 0:D],
                                                ALU.mult).then_inc(a_done, 1)

                    def gate(s, j, first):
                        b = j % 2
                        dve.wait_ge(w2_done, s + 1)
                        dve.wait_ge(sig_done, s + 1)
                        if not first:
                            dve.wait_ge(added, s - 1)
                        nc.vector.tensor_tensor(msg[b][:, :, :], mp[b][:, :].rearrange("p (t c) -> p t c", t=HALF),
                                                sig[b][:, :, D:2 * D], ALU.mult).then_inc(msg_done, 1)

                    def add_window(c):
                        dve.wait_ge(added, 2 * c + 2)
                        base = dve.value_load(base_i[0:1, ds(c, 1)], min_val=0, max_val=LAST_BASE)
                        to = sums[:, :, ds(base, WINDOW)]
                        if not (isinstance(c, int) and c == 0):
                            dve.wait_ge(sums_done, c)
                        nc.vector.tensor_tensor(to, to, sp_[:, 0:2 * WINDOW].rearrange("p (k n) -> p k n", k=2),
                                                ALU.add).then_inc(sums_done, 1)

                    def steps(i, first=False, last=False):
                        for j in range(4):
                            s, c = 4 * i + j, 2 * i + j // 2
                            z_add(s, j, i + 1, first and j < 2)
                            if j == 1 or (j == 3 and not last):
                                hot_rows(c + 1, (j // 2 + 1) % 2, i + 1 + j // 2, first and j == 1)
                            if j % 2 == 0:
                                hot_cols(c, j // 2, first)
                            a_mul(s, j, first and j < 2)
                            if j % 2 and not (first and j == 1):
                                add_window(c - 1)
                            if not (first and j == 0):
                                gate(s - 1, (j - 1) % 4, first and j <= 2)
                            if j % 2:
                                hot_sum(c, j // 2, first)

                    hot_rows(0, 0, 1, True)
                    steps(0, first=True)
                    with dve.Fori(1, ROUNDS - 1) as i:
                        steps(i)
                    steps(ROUNDS - 1, last=True)
                    gate(4 * ROUNDS - 1, 3, False)
                    add_window(CHUNKS - 1)
                    dve.wait_ge(sums_done, CHUNKS)

                def general():
                    with dve.Fori(0, CHUNKS) as c:
                        for t in range(TILES):
                            n = TILES * c + t + 1
                            dve.wait_ge(g_z, n)
                            dve.wait_ge(g_rows, 32 * n)
                            nc.vector.tensor_tensor(z[0][:, 1, :], zp[0][:, 0:2 * D], gath[0][:, 0, :], ALU.add) \
                                .then_inc(g_v, 1)
                            dve.wait_ge(g_v, (WIDES + 2) * (n - 1) + 1)
                            nc.vector.tensor_tensor(z[0][:, 0, :], z[0][:, 1, :], gath[0][:, 1, :], ALU.add) \
                                .then_inc(g_zs, 1)
                            dve.wait_ge(g_sig, n)
                            nc.vector.tensor_tensor(act_in[0][:, 0, :], z[0][:, 0, 0:D], sig[0][:, 0, 0:D], ALU.mult) \
                                .then_inc(g_a, 1)
                            dve.wait_ge(g_w2, n)
                            nc.vector.tensor_tensor(msg[0][:, 0, :], mp[0][:, 0:D], sig[0][:, 0, D:2 * D], ALU.mult) \
                                .then_inc(g_msg, 1)
                            nc.vector.tensor_copy(rel_w, dcol[:, ds(c * TILES + t, 1)]).then_inc(g_v, 1)
                            with dve.Fori(0, WIDES) as w:
                                done = (WIDES + 2) * (n - 1) + 2 + w
                                dve.wait_ge(g_v, done)
                                nc.vector.tensor_scalar(hot_w, iota_w, rel_w, None, ALU.is_equal).then_inc(g_hot, 1)
                                dve.wait_ge(g_hot, WIDES * (n - 1) + w + 1)
                                nc.vector.tensor_scalar(rel_w, rel_w, -float(WIDE), None, ALU.add).then_inc(g_v, 1)
                                dve.wait_ge(g_sum, WIDES * (n - 1) + w + 1)
                                to = sums[:, 0, ds(w * WIDE, WIDE)]
                                nc.vector.tensor_tensor(to, to, zp[1][:, 0:WIDE], ALU.add).then_inc(g_added, 1)
                                to = sums[:, 1, ds(w * WIDE, WIDE)]
                                nc.vector.tensor_tensor(to, to, zp[1][:, WIDE:2 * WIDE], ALU.add).then_inc(g_added, 1)
                                dve.wait_ge(g_added, 2 * (WIDES * (n - 1) + w + 1))
                            dve.wait_ge(g_v, (WIDES + 2) * n)
                            dve.sem_inc(g_start, 1)

                nodes_dve(dve)
                dve.wait_ge(h_tr, QUADS)
                dve.wait_ge(zeroed, 2)
                branches(dve, general, windowed)
                dve.sem_inc(edges_done, 1)
                update_dve(dve)

            @block.tensor
            def _(pe):
                def windowed():
                    def transposes(s, j, first):
                        pe.wait_ge(a_done, s + 1)
                        if not first:
                            pe.wait_ge(aT_done, s)
                        for t in range(HALF):
                            last = nc.tensor.transpose(tp[:, t * P:(t + 1) * P], act_in[j % 2][:, t, :], ident[:, :])
                        last.then_inc(tr_done, 1)

                    def z_products(s, c, j, round_end, first):
                        k, b = j // 2, j % 2
                        if b == 0:
                            pe.wait_ge(lhs_in[k], 32 * round_end)
                            pe.wait_ge(hotT_done, c + 1)
                        if not first:
                            pe.wait_ge(z_sum, s - 1)
                        for t in range(HALF):
                            e0 = (b * HALF + t) * P
                            last = nc.tensor.matmul(zp[b][:, t * 2 * D:(t + 1) * 2 * D], lhs[k][:, e0:e0 + P],
                                                    rhs[k][:, :], start=(t % 2 == 0), stop=True, skip_group_check=True)
                        last.then_inc(z_done, 1)

                    def w2_products(s, j, first):
                        b = j % 2
                        pe.wait_ge(aT_done, s + 1)
                        if not first:
                            pe.wait_ge(msg_done, s - 1)
                        bias(mp[b][:, :], 0, HALF * D)
                        for t in range(HALF):
                            last = nc.tensor.matmul(mp[b][:, t * D:(t + 1) * D], act_T[b][:, t * P:(t + 1) * P],
                                                    w2_sb, start=False, stop=True, skip_group_check=True)
                        last.then_inc(w2_done, 1)

                    def add_messages(s, c, j, first):
                        k, b = j // 2, j % 2
                        pe.wait_ge(msg_done, s + 1)
                        if b == 0:
                            pe.wait_ge(hot_done, c + 1)
                            if not first:
                                pe.wait_ge(sums_done, c)
                        for t in range(HALF):
                            last = nc.tensor.matmul(sp_[:, 0:WINDOW], msg[b][:, t, :], hot[k][:, b * HALF + t, :],
                                                    start=(b == 0 and t == 0), stop=True, skip_group_check=True)
                        if b == 1:
                            pe.wait_ge(count_done, c + 1)
                            last = nc.tensor.matmul(sp_[:, WINDOW:2 * WINDOW], ones_bf[:, :], count[k][:, :],
                                                    start=False, stop=True, skip_group_check=True)
                        last.then_inc(added, 1)

                    def steps(i, first):
                        for j in range(4):
                            s, c = 4 * i + j, 2 * i + j // 2
                            z_products(s, c, j, i + 1, first and j < 2)
                            if not (first and j == 0):
                                transposes(s - 1, (j - 1) % 4, first and j == 1)
                            if not (first and j < 2):
                                add_messages(s - 2, c - 1, (j - 2) % 4, first)
                            if not (first and j == 0):
                                w2_products(s - 1, (j - 1) % 4, first and j <= 2)

                    steps(0, True)
                    with pe.Fori(1, ROUNDS) as i:
                        steps(i, False)
                    s = 4 * ROUNDS
                    transposes(s - 1, 3, False)
                    add_messages(s - 2, CHUNKS - 1, 2, False)
                    w2_products(s - 1, 3, False)
                    add_messages(s - 1, CHUNKS - 1, 3, False)

                def general():
                    with pe.Fori(0, CHUNKS) as c:
                        pe.wait_ge(g_in, 48 * (c + 1))
                        for t in range(TILES):
                            n = TILES * c + t + 1
                            pe.wait_ge(g_start, n)
                            nc.tensor.matmul(zp[0][:, 0:2 * D], lhs[0][0:ED, t * P:(t + 1) * P], rhs[0][0:ED, :],
                                             start=True, stop=True).then_inc(g_z, 1)
                            pe.wait_ge(g_a, n)
                            nc.tensor.transpose(tp[:, 0:P], act_in[0][:, 0, :], ident[:, :]).then_inc(g_t, 1)
                            pe.wait_ge(g_aT, n)
                            bias(mp[0][:, 0:D], 0, D)
                            nc.tensor.matmul(mp[0][:, 0:D], act_T[0][:, 0:P], w2_sb, start=False, stop=True,
                                             skip_group_check=True) \
                                .then_inc(g_w2, 1)
                            pe.wait_ge(g_msg, n)
                            pe.sem_inc(g_windows, 1)
                            with pe.Fori(0, WIDES) as w:
                                pe.wait_ge(g_hot, WIDES * (n - 1) + w + 1)
                                nc.tensor.matmul(zp[1][:, 0:WIDE], msg[0][:, 0, :], hot_w, start=True, stop=True)
                                nc.tensor.matmul(zp[1][:, WIDE:2 * WIDE], ones[:, :], hot_w, start=True, stop=True) \
                                    .then_inc(g_sum, 1)

                nodes_pe(pe)
                pe.wait_ge(staged_dst, QUADS)
                pe.wait_ge(own_done, QUADS)
                branches(pe, general, windowed)
                update_pe(pe)


def kernel(**inputs):
    import numpy as np
    import concourse.bacc as bacc
    from concourse.bass_utils import run_bass_kernel_spmd as run

    edge = np.concatenate([np.arange((CHUNKS - 1) * CHUNK), np.arange(E - CHUNK, E)])
    src = np.asarray(inputs["src"])[edge].reshape(CHUNKS, TILES, P)
    dst = np.asarray(inputs["dst"])[edge].reshape(CHUNKS, TILES, P)
    e = np.asarray(inputs["edge_attr_64"])[edge].reshape(CHUNKS, CHUNK, ED)
    weight = {k: np.asarray(inputs["L0_gnn_" + k]) for k in ("w1", "b1", "w2", "b2", "wg", "bg", "wu", "bu")}
    arrays = {
        "x": inputs["x"],
        "src_ch": src.transpose(0, 2, 1),
        "dst_rows": dst.reshape(CHUNKS, CHUNK),
        "dst_cols": dst.transpose(2, 0, 1).reshape(P, CHUNKS * TILES),
        "dst_first": dst[:, 0, 0].reshape(1, CHUNKS),
        "e_ch": e.transpose(0, 2, 1),
        "w_z": np.concatenate([weight["w1"], weight["wg"]], axis=1),
        "w_sq": np.concatenate([weight["w2"], weight["wu"]], axis=0),
        "biases": np.concatenate([weight[k] for k in ("b1", "bg", "b2", "bu")])[None],
    }
    nc = bacc.Bacc("TRN2", target_bir_lowering=False, num_devices=1)
    args, maps = [], {}
    for name, a in arrays.items():
        a = np.ascontiguousarray(a)
        maps[f"in_{name}"] = a
        args.append(nc.dram_tensor(f"in_{name}", a.shape, mybir.dt.from_np(a.dtype), kind="ExternalInput").ap())
    args.append(nc.dram_tensor("out", (N, D), mybir.dt.float32, kind="ExternalOutput").ap())
    gnn_program(nc, *args)
    return run(nc, [maps], core_ids=[0]).results[0]["out"]
```

```python
import concourse.bass as bass
from concourse import mybir
from contextlib import ExitStack

N, E, D, ED = 6250, 200000, 128, 64
P = 128
TILES = 8
HALF = TILES // 2
CHUNK = TILES * P
CHUNKS = -(-E // CHUNK)
REPEATED = CHUNKS * CHUNK - E
ROUNDS = CHUNKS // 2
WINDOW = 64
LAST_BASE = N - WINDOW
NTILES = -(-N // P)
NODE_REPEATED = NTILES * P - N
WIDE = 512
WIDES = -(-N // WIDE)
NPAD = WIDES * WIDE
FOREIGN = -1.0e6
EPS = 1e-5
QUAD = 4
QUADS = -(-NTILES // QUAD)
STATS = [0, 8, 20, 32, NTILES]
OWN_EARLY = QUADS - 5
OWN_FILL = QUADS - 4
DEGREES = [0, 2, 6, QUADS]
assert CHUNKS % 2 == 0


def node_start(t):
    return min(t * P, N - P)


def quad_tiles(q):
    return range(QUAD * q, min(QUAD * (q + 1), NTILES))


def gnn_program(nc, x, src_ch, dst_rows, dst_cols, dst_first, e_ch, w_z, w_sq, biases, out):
    fp32, bf16, i32 = mybir.dt.float32, mybir.dt.bfloat16, mybir.dt.int32
    ALU = mybir.AluOpType
    ACT = mybir.ActivationFunctionType
    AX = mybir.AxisListType.X
    ds = bass.ds

    src_table = nc.dram_tensor("src_table", [N, 2 * D], fp32, kind="Internal").ap()
    dst_table = nc.dram_tensor("dst_table", [N, 2 * D], fp32, kind="Internal").ap()
    src_rows2 = src_ch.rearrange("c p t -> (c p) t")
    e_rows = e_ch.rearrange("c f n -> (c f) n")

    ctx = ExitStack()
    with ctx:
        def sb(name, shape, dt=fp32):
            return ctx.enter_context(nc.sbuf_tensor(name, shape, dt))

        def pb(name, shape):
            return ctx.enter_context(nc.psum_tensor(name, shape, fp32))

        def sem(name):
            return ctx.enter_context(nc.semaphore(name))

        xs = sb("xs", [P, NTILES, D])
        hT = sb("hT", [P, NTILES, P])
        sums = sb("sums", [P, 2, NPAD])
        own = hT
        bn = sb("bn", [P, NTILES, 6])
        stat = sb("stat", [P, 4, NTILES])
        degree = sb("degree", [P, NTILES])
        w_node = sb("w_node", [P, 4 * D])
        w_square = sb("w_square", [P, 3, D])
        w2_sb, wu_h, wu_mean = (w_square[:, k, :] for k in range(3))
        b_all = sb("b_all", [P, 4, D])
        b_rest = sb("b_rest", [P, 2, D])
        b_parts = sb("b_parts", [P, 2, QUAD, D], bf16)
        ident = sb("ident", [P, P])
        ones_bf = sb("ones_bf", [P, P], bf16)
        ones = sb("ones", [P, P])
        iota_i = sb("iota_i", [P, WIDE], i32)
        iota_f = sb("iota_f", [P, WIDE])
        row_i = sb("row_i", [P, 1], i32)
        row_f = sb("row_f", [P, 1])
        dcol_i = sb("dcol_i", [P, CHUNKS * TILES], i32)
        dcol = sb("dcol", [P, CHUNKS * TILES])
        drel = sb("drel", [P, CHUNKS * TILES])
        first_i = sb("first_i", [P, CHUNKS], i32)
        base_i = sb("base_i", [P, CHUNKS], i32)
        base_f = sb("base_f", [P, CHUNKS])
        own_node = sb("own_node", [P, CHUNKS])
        outside = sb("outside", [P, 2])
        flag_i = sb("flag_i", [1, 1], i32)
        lhs = [sb(f"lhs{k}", [P, CHUNK]) for k in range(2)]
        rhs = [sb(f"rhs{k}", [P, 2 * D]) for k in range(2)]
        dst_row = [sb(f"dst_row{k}", [P, CHUNK], i32) for k in range(2)]
        idx = [sb(f"idx{k}", [P, TILES], i32) for k in range(2)]
        gath = [sb(f"gath{k}", [P, TILES, 2 * D]) for k in range(2)]
        z = [sb(f"z{k}", [P, HALF, 2 * D]) for k in range(2)]
        sig = [sb(f"sig{k}", [P, HALF, 2 * D]) for k in range(2)]
        act_in = [sb(f"a{k}", [P, HALF, D]) for k in range(2)]
        act_T = [sb(f"aT{k}", [P, HALF * P]) for k in range(2)]
        msg = [sb(f"msg{k}", [P, HALF, D]) for k in range(2)]
        hot = [sb(f"hot{k}", [P, TILES, WINDOW]) for k in range(2)]
        count = [sb(f"count{k}", [P, WINDOW], bf16) for k in range(2)]
        def flat(a):
            return a[:, :, :].rearrange("p t c -> p (t c)")

        normed = [act_in[0], act_in[1], msg[0], msg[1]]
        stage_src = [flat(gath[k // 2])[:, (k % 2) * 1024:(k % 2 + 1) * 1024] for k in range(4)]
        stage_dst = [flat(z[0]), flat(z[1]), flat(sig[0]), flat(sig[1])]

        zp = [pb(f"zp{k}", [P, HALF * 2 * D]) for k in range(2)]
        tp = pb("tp", [P, 512])
        mp = [pb(f"mp{k}", [P, 512]) for k in range(2)]
        sp_ = pb("sum_p", [P, 512])

        x_in = [sem(f"x_in{q}") for q in range(QUADS)]
        w_in = sem("w_in")
        edge_w_in = sem("edge_w_in")
        d_in = sem("d_in")
        pool_chain = sem("pool_chain")
        made = sem("made")
        prepared = sem("prepared")
        zeroed = sem("zeroed")
        dve_chain = sem("dve_chain")
        b2_done = sem("b2_done")
        bn_done = sem("bn_done")
        var_done = sem("var_done")
        dev_done = sem("dev_done")
        normed_done = sem("normed_done")
        h_tr = sem("h_tr")
        hT_done = sem("hT_done")
        tab_src = sem("tab_src")
        tab_dst = sem("tab_dst")
        own_up = sem("own_up")
        own_done = sem("own_done")
        staged_src = sem("staged_src")
        staged_dst = sem("staged_dst")
        src_stored = [sem(f"src_stored{k}") for k in range(4)]
        dst_stored = [sem(f"dst_stored{k}") for k in range(4)]
        windows_checked = sem("windows_checked")
        outside_sum = sem("outside_sum")
        flag_done = sem("flag_done")

        def all_stored(eng, stored):
            for k in range(4):
                eng.wait_ge(stored[k], 16 * len(range(k, QUADS, 4)))

        def load_x(sp):
            for q in range(QUADS - 1):
                t0 = QUAD * q
                sp.dma_start(xs[:, t0:t0 + QUAD, :], x[t0 * P:(t0 + QUAD) * P, :].rearrange("(t p) d -> p t d", p=P)) \
                    .then_inc(x_in[q], 16)
            sp.dma_start(xs[:, NTILES - 1, :], x[N - P:N, :]).then_inc(x_in[-1], 16)

        def store_tables(sp):
            for table, staged, stage, stored in ((src_table, staged_src, stage_src, src_stored),
                                                 (dst_table, staged_dst, stage_dst, dst_stored)):
                for q in range(QUADS):
                    sp.wait_ge(staged, q + 1)
                    if len(quad_tiles(q)) == QUAD:
                        n0 = q * QUAD * P
                        sp.dma_start(table[n0:n0 + QUAD * P, :].rearrange("(t p) c -> p t c", p=P),
                                     stage[q % 4].rearrange("p (t c) -> p t c", t=QUAD)).then_inc(stored[q % 4], 16)
                    else:
                        sp.dma_start(table[N - P + NODE_REPEATED:N, :], stage[q % 4][NODE_REPEATED:P, 0:2 * D]) \
                            .then_inc(stored[q % 4], 16)

        def prepare(pool):
            links = [0]

            def link(ins):
                links[0] += 1
                ins.then_inc(pool_chain, 1)
                pool.wait_ge(pool_chain, links[0])

            link(pool.memset(ident[:, :], 0.0))
            pool.affine_select(out=ident[:, :], in_=ident[:, :], compare_op=ALU.not_equal, fill=1.0,
                               base=0, pattern=[[-1, P]], channel_multiplier=1).then_inc(made, 1)
            pool.memset(ones_bf[:, :], 1.0).then_inc(made, 1)
            pool.memset(ones[:, :], 1.0).then_inc(made, 1)
            pool.iota(iota_i[:, :], pattern=[[1, WIDE]], base=0, channel_multiplier=0).then_inc(pool_chain, 1)
            pool.iota(row_i[:, :], pattern=[[0, 1]], base=-WINDOW, channel_multiplier=1).then_inc(pool_chain, 1)
            links[0] += 2
            pool.wait_ge(pool_chain, links[0])
            pool.tensor_copy(iota_f[:, :], iota_i[:, :]).then_inc(prepared, 1)
            link(pool.tensor_copy(row_f[:, :], row_i[:, :]))
            pool.wait_ge(d_in, 32)
            link(pool.tensor_scalar(base_f[:, :], first_i[:, :], float(LAST_BASE), None, ALU.min))
            pool.tensor_copy(base_i[:, :], base_f[:, :]).then_inc(prepared, 1)
            pool.tensor_scalar(own_node[:, :], base_f[:, :], row_f[:, 0:1], None, ALU.add).then_inc(prepared, 1)
            link(pool.tensor_copy(dcol[:, :], dcol_i[:, :]))
            link(pool.tensor_tensor(drel[:, :].rearrange("p (c t) -> p c t", t=TILES),
                                    dcol[:, :].rearrange("p (c t) -> p c t", t=TILES),
                                    base_f[:, :].unsqueeze(2).to_broadcast([P, CHUNKS, TILES]), ALU.subtract))
            pool.sem_inc(prepared, 1)
            pool.memset(sums[:, 0, :], 0.0).then_inc(zeroed, 1)
            pool.memset(sums[:, 1, :], 0.0).then_inc(zeroed, 1)

        def check_windows(dve):
            dve.wait_ge(prepared, 4)
            dve_link(dve, nc.vector.tensor_reduce(outside[:, 0:1], drel[:, :], AX, ALU.min))
            dve_link(dve, nc.vector.tensor_reduce(outside[:, 1:2], drel[:, :], AX, ALU.max))
            dve_link(dve, nc.vector.tensor_scalar(outside[:, 0:1], outside[:, 0:1], 0.0, None, ALU.is_lt))
            dve_link(dve, nc.vector.tensor_scalar(outside[:, 1:2], outside[:, 1:2], float(WINDOW - 1), None, ALU.is_gt))
            c0 = (CHUNKS - 1) * TILES
            full, rest = REPEATED // P, REPEATED % P
            for m in (drel, dcol):
                dve_link(dve, nc.vector.memset(m[:, c0:c0 + full], FOREIGN))
                if rest:
                    dve_link(dve, nc.vector.memset(m[0:rest, c0 + full:c0 + full + 1], FOREIGN))
            dve.sem_inc(windows_checked, 1)

        dve_links = [0]

        def dve_link(dve, ins):
            dve_links[0] += 1
            ins.then_inc(dve_chain, 1)
            dve.wait_ge(dve_chain, dve_links[0])

        def load_weights(act):
            act.dma_start(w_node[:, :].rearrange("p (k c) -> p k c", k=2),
                          w_z[0:2 * D, :].rearrange("(k p) c -> p k c", p=P)).then_inc(w_in, 16)
            act.dma_start(first_i[:, :], dst_first[:, :].to_broadcast([P, CHUNKS])).then_inc(d_in, 16)
            act.dma_start(dcol_i[:, :], dst_cols[:, :]).then_inc(d_in, 16)

        def load_edge_weights(sp):
            sp.dma_start(b_all[:, :, :].rearrange("p k d -> p (k d)"), biases[:, :].to_broadcast([P, 4 * D])) \
                .then_inc(edge_w_in, 16)
            sp.dma_start(w_square[:, :, :], w_sq.rearrange("(k p) d -> p k d", p=P)).then_inc(edge_w_in, 16)
            for to in rhs:
                sp.dma_start(to[0:ED, :], w_z[2 * D:2 * D + ED, :]).then_inc(edge_w_in, 16)

        W_NODE, W_EDGE = 16, 16 * 4

        def nodes_act(act):
            def deviation(g):
                act.wait_ge(var_done, g + 1)
                s = slice(STATS[g], STATS[g + 1])
                nc.scalar.activation(stat[:, 2, s], stat[:, 1, s], ACT.Sqrt).then_inc(dev_done, 1)

            def src_rows(q):
                w = len(quad_tiles(q)) * 2 * D
                act.wait_ge(tab_src, q + 1)
                if q >= 4:
                    act.wait_ge(src_stored[q % 4], 16 * (q // 4))
                nc.scalar.copy(stage_src[q % 4][:, 0:w], zp[q % 2][:, 0:w]).then_inc(staged_src, 1)

            deviation(0)
            for q in range(QUADS):
                w = len(quad_tiles(q)) * P
                if QUAD * (q + 1) in STATS[2:-1]:
                    deviation(STATS.index(QUAD * (q + 1)))
                act.wait_ge(h_tr, q + 1)
                nc.scalar.activation(hT[:, QUAD * q:QUAD * q + w // P, :].rearrange("p t n -> p (t n)"), mp[q % 2][:, 0:w],
                                     ACT.Relu).then_inc(hT_done, 1)
                if QUAD * (q + 1) == STATS[1]:
                    deviation(1)
                if q >= 1:
                    src_rows(q - 1)
            src_rows(QUADS - 1)
            own_rows(act, 0, OWN_EARLY)

        def own_bank(q):
            if q < OWN_FILL:
                return mp[q % 2][:, :]
            late = q - OWN_FILL
            return zp[late // 2][:, late % 2 * QUAD * D:(late % 2 + 1) * QUAD * D]

        def own_rows(act, q0, q1):
            for q in range(q0, q1):
                w = len(quad_tiles(q)) * D
                act.wait_ge(own_up, q + 1)
                nc.scalar.copy(own[:, QUAD * q:QUAD * q + w // D, :].rearrange("p t d -> p (t d)"), own_bank(q)[:, 0:w]) \
                    .then_inc(own_done, 1)

        def nodes_dve(dve):
            def moments(g):
                a, b = STATS[g], STATS[g + 1]
                for t in range(a, b):
                    if t % QUAD == 0:
                        dve.wait_ge(x_in[t // QUAD], 16)
                    last = nc.vector.bn_stats(bn[:, t, :], xs[:, t, :])
                last.then_inc(bn_done, 1)

            def variance(g):
                a, b = STATS[g], STATS[g + 1]
                even, odd = bn[:, a:b, 1], bn[:, a:b, 4]
                mean, var, scr = stat[:, 0, a:b], stat[:, 1, a:b], stat[:, 3, a:b]
                dve.wait_ge(bn_done, g + 1)
                nc.vector.tensor_tensor(mean, even, odd, ALU.add)
                nc.vector.tensor_tensor(var, bn[:, a:b, 2], bn[:, a:b, 5], ALU.add)
                dve_link(dve, nc.vector.tensor_tensor(scr, even, odd, ALU.subtract))
                nc.vector.tensor_scalar(mean, mean, 0.5, None, ALU.mult)
                nc.vector.tensor_scalar(var, var, 1.0 / D, EPS, ALU.mult, ALU.add)
                dve_link(dve, nc.vector.scalar_tensor_tensor(scr, scr, 0.25, scr, ALU.mult, ALU.mult))
                nc.vector.tensor_tensor(var, var, scr, ALU.add).then_inc(var_done, 1)

            def normalise(g):
                a, b = STATS[g], STATS[g + 1]
                dve.wait_ge(dev_done, g + 1)
                dve_link(dve, nc.vector.reciprocal(stat[:, 2, a:b], stat[:, 2, a:b]))
                for q in range(a // QUAD, -(-b // QUAD)):
                    if q >= 4:
                        dve.wait_ge(h_tr, q - 3)
                    for t in quad_tiles(q):
                        last = nc.vector.tensor_scalar(normed[q % 4][:, t % QUAD, :], xs[:, t, :], stat[:, 0, t:t + 1],
                                                       stat[:, 2, t:t + 1], ALU.subtract, ALU.mult)
                    last.then_inc(normed_done, 1)

            for g in range(len(STATS) - 1):
                moments(g)
                variance(g)
                normalise(g)
            check_windows(dve)
            dve.wait_ge(edge_w_in, W_EDGE)
            dve_link(dve, nc.vector.memset(b_parts[:, :, :, :], 0.0))
            for row in (0, 32, 64):
                at = slice(row, row + 1)
                whole, rest = b_all[at, 2:4, :], b_rest[at, :, :]
                part = b_parts[at, :, 0, :]
                dve_link(dve, nc.vector.tensor_copy(part, whole))
                if row >= 32:
                    dve_link(dve, nc.vector.tensor_tensor(rest, whole, part, ALU.subtract))
                    dve_link(dve, nc.vector.tensor_copy(part, rest))
                if row == 64:
                    dve_link(dve, nc.vector.tensor_tensor(whole, rest, part, ALU.subtract))
                    dve_link(dve, nc.vector.tensor_copy(part, whole))
            for j in range(1, QUAD):
                ins = nc.vector.tensor_copy(b_parts[:, :, j, :], b_parts[:, :, 0, :])
                ins.then_inc(b2_done, 1)
            dve.wait_ge(outside_sum, 1)
            nc.vector.tensor_copy(flag_i[:, :], tp[0:1, 0:1]).then_inc(flag_done, 1)
            for q in range(QUADS):
                tiles = len(quad_tiles(q))
                dve.wait_ge(tab_dst, q + 1)
                if q >= 4:
                    dve.wait_ge(dst_stored[q % 4], 16 * (q // 4))
                nc.vector.tensor_tensor(stage_dst[q % 4][:, 0:tiles * 2 * D].rearrange("p (t c) -> p t c", t=tiles),
                                        zp[(QUADS + q) % 2][:, 0:tiles * 2 * D].rearrange("p (t c) -> p t c", t=tiles),
                                        b_all[:, 0:2, :].rearrange("p k d -> p (k d)").unsqueeze(1)
                                        .to_broadcast([P, tiles, 2 * D]),
                                        ALU.add).then_inc(staged_dst, 1)

        def bias(to, which, width):
            nc.tensor.matmul(to, ones_bf[:, :], b_parts[:, which, 0:width // D, :].rearrange("p t d -> p (t d)"),
                             start=True, stop=True, skip_group_check=True)

        def nodes_pe(pe):
            def products(q, bank, side, done):
                for t in quad_tiles(q):
                    last = nc.tensor.matmul(zp[bank][:, (t % QUAD) * 2 * D:(t % QUAD + 1) * 2 * D], hT[:, t, :],
                                            w_node[:, side * 2 * D:(side + 1) * 2 * D], start=(t % 2 == 0), stop=True,
                                            skip_group_check=True)
                last.then_inc(done, 1)

            def src_products(q):
                pe.wait_ge(hT_done, q + 1)
                if q >= 2:
                    pe.wait_ge(staged_src, q - 1)
                products(q, q % 2, 0, tab_src)

            pe.wait_ge(made, 3)
            with pe.Fori(0, 8) as _:
                for k in range(3):
                    nc.tensor.transpose(tp[:, k * P:(k + 1) * P], ident[:, :], ident[:, :])
            pe.wait_ge(w_in, W_NODE)
            for q in range(QUADS):
                pe.wait_ge(normed_done, q + 1)
                if q >= 2:
                    pe.wait_ge(hT_done, q - 1)
                for t in quad_tiles(q):
                    last = nc.tensor.transpose(mp[q % 2][:, (t % QUAD) * P:(t % QUAD + 1) * P],
                                               normed[q % 4][:, t % QUAD, :], ident[:, :])
                last.then_inc(h_tr, 1)
                if q >= 1:
                    src_products(q - 1)
            src_products(QUADS - 1)
            pe.wait_ge(windows_checked, 1)
            nc.tensor.matmul(tp[0:1, 0:1], outside[:, 0:1], ones[:, 0:1], start=True, stop=False)
            nc.tensor.matmul(tp[0:1, 0:1], outside[:, 1:2], ones[:, 0:1], start=False, stop=True) \
                .then_inc(outside_sum, 1)
            for q in range(QUADS):
                bank = (QUADS + q) % 2
                if q < 2:
                    pe.wait_ge(staged_src, QUADS - 1 + q)
                else:
                    pe.wait_ge(staged_dst, q - 1)
                products(q, bank, 1, tab_dst)
            pe.wait_ge(edge_w_in, W_EDGE)
            pe.wait_ge(b2_done, QUAD - 1)
            own_to_rows(pe, 0, OWN_EARLY)

        def own_products(q):
            w, to = len(quad_tiles(q)) * D, own_bank(q)
            bias(to[:, 0:w], 1, w)
            for t in quad_tiles(q):
                o = (t % QUAD) * D
                last = nc.tensor.matmul(to[:, o:o + D], hT[:, t, :], wu_h, start=False, stop=True, skip_group_check=True)
            last.then_inc(own_up, 1)

        def own_to_rows(pe, q0, q1):
            for q in range(q0, q1):
                if q >= 2:
                    pe.wait_ge(own_done, q - 1)
                own_products(q)

        lhs_in = [sem(f"lhs_in{k}") for k in range(2)]
        dst_in = [sem(f"dst_in{k}") for k in range(2)]
        idx_in = [sem(f"idx_in{k}") for k in range(2)]
        gathered = [sem(f"gathered{j}") for j in range(4)]
        opened = sem("opened")
        hotT_done = sem("hotT_done")
        hot_done = sem("hot_done")
        count_done = sem("count_done")
        z_done = sem("z_done")
        z_sum = sem("z_sum")
        sig_done = sem("sig_done")
        a_done = sem("a_done")
        tr_done = sem("tr_done")
        aT_done = sem("aT_done")
        w2_done = sem("w2_done")
        msg_done = sem("msg_done")
        added = sem("added")
        sums_done = sem("sums_done")

        edges_done = sem("edges_done")

        g_start = sem("g_start")
        g_in = sem("g_in")
        g_rows = sem("g_rows")
        g_z = sem("g_z")
        g_zs = sem("g_zs")
        g_sig = sem("g_sig")
        g_a = sem("g_a")
        g_t = sem("g_t")
        g_aT = sem("g_aT")
        g_w2 = sem("g_w2")
        g_msg = sem("g_msg")
        g_hot = sem("g_hot")
        g_sum = sem("g_sum")
        g_v = sem("g_v")
        g_added = sem("g_added")
        g_windows = sem("g_windows")
        gdst = dst_row[0][:, 0:TILES]
        iota_w = iota_f[:, :]
        hot_w = hot[1].rearrange("p t n -> p (t n)")[:, 0:WIDE]
        rel_w = outside[:, 0:1]

        def branches(eng, general, windowed):
            eng.wait_ge(flag_done, 1)
            general_case = eng.value_load(flag_i[0:1, 0:1], min_val=0, max_val=2 * P)
            with eng.If(general_case > 0):
                general()
            with eng.Else():
                windowed()
            eng.nop()

        SPARE = 8
        degree_T = sem("degree_T")
        degree_up = sem("degree_up")
        share_done = sem("share_done")
        up_done = sem("up_done")
        up_sum = sem("up_sum")
        silu_done = sem("silu_done")
        final_done = sem("final_done")
        out_stored = [sem(f"out_stored{k}") for k in range(4)]
        u_in = [flat(z[k])[:, 0:QUAD * D] for k in range(2)]
        u_silu = [flat(sig[k])[:, 0:QUAD * D] for k in range(2)]
        u_out = [flat(gath[0])[:, k * QUAD * D:(k + 1) * QUAD * D] for k in range(4)]

        def update_pe(pe):
            def degrees(g):
                if g >= 2:
                    pe.wait_ge(share_done, g - 1)
                for t in range(QUAD * DEGREES[g], min(QUAD * DEGREES[g + 1], NTILES)):
                    n0, o = node_start(t), (t - QUAD * DEGREES[g]) * SPARE
                    last = nc.tensor.transpose((tp, sp_)[g % 2][:, o:o + SPARE], sums[0:SPARE, 1, n0:n0 + P],
                                               ident[0:SPARE, 0:SPARE])
                last.then_inc(degree_T, 1)

            pe.wait_ge(edges_done, 1)
            for q in range(QUADS):
                if q in DEGREES:
                    degrees(DEGREES.index(q))
                if q >= 2:
                    pe.wait_ge(up_sum, q - 1)
                for t in quad_tiles(q):
                    n0, o = node_start(t), (t % QUAD) * D
                    last = nc.tensor.matmul(mp[q % 2][:, o:o + D], sums[:, 0, n0:n0 + P], wu_mean, start=True, stop=True,
                                            skip_group_check=True)
                last.then_inc(up_done, 1)

        def update_dve(dve):
            def shares(g):
                a, b = QUAD * DEGREES[g], min(QUAD * DEGREES[g + 1], NTILES)
                dve.wait_ge(degree_T, g + 1)
                nc.vector.tensor_scalar(degree[:, a:b],
                                        (tp, sp_)[g % 2][:, 0:(b - a) * SPARE]
                                        .rearrange("p (t k) -> p t k", k=SPARE)[:, :, 0],
                                        1.0, None, ALU.max).then_inc(degree_up, 1)
                dve.wait_ge(degree_up, g + 1)
                nc.vector.reciprocal(degree[:, a:b], degree[:, a:b]).then_inc(share_done, 1)
                dve.wait_ge(share_done, g + 1)

            for q in range(QUADS):
                if q in DEGREES:
                    shares(DEGREES.index(q))
                dve.wait_ge(up_done, q + 1)
                dve.wait_ge(own_done, q + 1)
                if q >= 2:
                    dve.wait_ge(silu_done, q - 1)
                for t in quad_tiles(q):
                    o = (t % QUAD) * D
                    last = nc.vector.scalar_tensor_tensor(
                        u_in[q % 2][:, o:o + D], mp[q % 2][:, o:o + D], degree[:, t:t + 1],
                        own[:, t, :], ALU.mult, ALU.add)
                last.then_inc(up_sum, 1)

        def update_act(act):
            own_rows(act, OWN_FILL, QUADS)
            for q in range(QUADS):
                b, w = q % 2, len(quad_tiles(q)) * D
                act.wait_ge(up_sum, q + 1)
                if q >= 2:
                    act.wait_ge(final_done, q - 1)
                nc.scalar.activation(u_silu[b][:, 0:w], u_in[b][:, 0:w], ACT.Silu).then_inc(silu_done, 1)

        def update_pool(pool):
            for q in range(QUADS):
                tiles = len(quad_tiles(q))
                w = tiles * D
                pool.wait_ge(silu_done, q + 1)
                if q >= 4:
                    pool.wait_ge(out_stored[q % 4], 16 * (q // 4))
                pool.tensor_tensor(u_out[q % 4][:, 0:w], u_silu[q % 2][:, 0:w],
                                   xs[:, QUAD * q:QUAD * q + tiles, :].rearrange("p t d -> p (t d)"),
                                   ALU.add).then_inc(final_done, 1)

        def store_out(sp):
            for q in range(QUADS):
                sp.wait_ge(final_done, q + 1)
                if len(quad_tiles(q)) == QUAD:
                    n0 = QUAD * q * P
                    sp.dma_start(out[n0:n0 + QUAD * P, :].rearrange("(t p) d -> p t d", p=P),
                                 u_out[q % 4][:, :].rearrange("p (t d) -> p t d", d=D)).then_inc(out_stored[q % 4], 16)
                else:
                    sp.dma_start(out[N - P + NODE_REPEATED:N, :], u_out[q % 4][NODE_REPEATED:P, 0:D]) \
                        .then_inc(out_stored[q % 4], 16)
            for k in range(4):
                sp.wait_ge(out_stored[k], 16 * len(range(k, QUADS, 4)))

        with nc.Block() as block:

            @block.sync
            def _(sp):
                def load_edges(c, k):
                    sp.dma_start(dst_row[k][WINDOW:P, :], dst_rows[ds(c, 1), :].to_broadcast([WINDOW, CHUNK])) \
                        .then_inc(dst_in[k], 16)
                    sp.dma_start(lhs[k][0:ED, :], e_rows[ds(c * ED, ED), :]).then_inc(lhs_in[k], 16)

                def load_indices(c, k):
                    sp.dma_start(idx[k][:, :], src_rows2[ds(c * P, P), :]).then_inc(idx_in[k], 16)

                def window_base(c):
                    return sp.value_load(base_i[0:1, ds(c, 1)], min_val=0, max_val=LAST_BASE)

                def load_window(base, k):
                    sp.dma_start(rhs[k][WINDOW:P, :], dst_table[ds(base, WINDOW), :]).then_inc(lhs_in[k], 16)

                def windowed():
                    def load(i, k):
                        c = 2 * i + k
                        for j in (2 * k, 2 * k + 1):
                            sp.wait_ge(gathered[j], 64 * i)
                        load_indices(c, k)
                        sp.wait_ge(z_done, 2 * c - 2)
                        load_edges(c, k)
                        load_window(window_base(c), k)

                    bases = [window_base(k) for k in range(2)]
                    all_stored(sp, dst_stored)
                    for k in range(2):
                        load_window(bases[k], k)
                    with sp.Fori(1, ROUNDS) as i:
                        for k in range(2):
                            load(i, k)

                def general():
                    all_stored(sp, dst_stored)
                    for k in range(2):
                        sp.wait_ge(idx_in[k], 16)
                        sp.wait_ge(dst_in[k], 16)
                        sp.wait_ge(lhs_in[k], 16)
                    with sp.Fori(0, CHUNKS) as c:
                        sp.wait_ge(g_start, TILES * c + 1)
                        sp.dma_start(idx[0][:, :], src_rows2[ds(c * P, P), :]).then_inc(g_in, 16)
                        sp.dma_start(gdst, dst_cols[:, ds(c * TILES, TILES)]).then_inc(g_in, 16)
                        sp.dma_start(lhs[0][0:ED, :], e_rows[ds(c * ED, ED), :]).then_inc(g_in, 16)

                load_x(sp)
                for k in range(2):
                    load_indices(k, k)
                    load_edges(k, k)
                load_edge_weights(sp)
                store_tables(sp)
                all_stored(sp, src_stored)
                sp.wait_ge(prepared, 4)
                branches(sp, general, windowed)
                store_out(sp)

            @block.gpsimd
            def _(pool):
                def gather(table, to, index):
                    return pool.indirect_dma_start(out=to, out_offset=None, in_=table[:, :],
                                                   in_offset=bass.IndirectOffsetOnAxis(ap=index, axis=0))

                def windowed():
                    def gathers(i, first):
                        for j in range(4):
                            k, h0 = j // 2, (j % 2) * HALF
                            if h0 == 0:
                                pool.wait_ge(idx_in[k], 16 * (i + 1))
                            if not first:
                                pool.wait_ge(z_sum, 4 * i + j - 3)
                            pool.sem_inc(opened, 1)
                            for t in range(h0, h0 + HALF):
                                pool.indirect_dma_start(
                                    out=gath[k][:, t, :], out_offset=None, in_=src_table[:, :],
                                    in_offset=bass.IndirectOffsetOnAxis(ap=idx[k][:, t:t + 1], axis=0)) \
                                    .then_inc(gathered[j], 16)

                    pool.wait_ge(staged_dst, 9)
                    gathers(0, True)
                    with pool.Fori(1, ROUNDS) as i:
                        gathers(i, False)

                def general():
                    pool.sem_inc(g_start, 1)
                    all_stored(pool, dst_stored)
                    with pool.Fori(0, CHUNKS) as c:
                        pool.wait_ge(g_in, 48 * (c + 1))
                        for t in range(TILES):
                            pool.wait_ge(g_start, TILES * c + t + 1)
                            pool.sem_inc(opened, 1)
                            gather(src_table, gath[0][:, 0, :], idx[0][:, t:t + 1]).then_inc(g_rows, 16)
                            gather(dst_table, gath[0][:, 1, :], gdst[:, t:t + 1]).then_inc(g_rows, 16)

                prepare(pool)
                all_stored(pool, src_stored)
                branches(pool, general, windowed)
                update_pool(pool)

            @block.scalar
            def _(act):
                def windowed():
                    def transposed(s, b, first):
                        act.wait_ge(tr_done, s + 1)
                        if not first:
                            act.wait_ge(w2_done, s - 1)
                        nc.scalar.copy(act_T[b][:, :], tp[:, :]).then_inc(aT_done, 1)

                    def sigmoids(s, b, first):
                        act.wait_ge(z_sum, s + 1)
                        if not first:
                            act.wait_ge(msg_done, s - 1)
                            act.wait_ge(a_done, s - 1)
                        nc.scalar.activation(sig[b][:, :, :], z[b][:, :, :], ACT.Sigmoid).then_inc(sig_done, 1)

                    def step(s, j, first):
                        b = j % 2
                        if not (first and j == 0):
                            transposed(s - 1, 1 - b, first and j <= 2)
                        sigmoids(s, b, first and j < 2)

                    for j in range(4):
                        step(j, j, True)
                        if j == 0:
                            own_rows(act, OWN_EARLY, OWN_FILL)
                    with act.Fori(1, ROUNDS) as i:
                        for j in range(4):
                            step(4 * i + j, j, False)
                    transposed(4 * ROUNDS - 1, 1, False)

                def general():
                    own_rows(act, OWN_EARLY, OWN_FILL)
                    with act.Fori(0, CHUNKS) as c:
                        for t in range(TILES):
                            n = TILES * c + t + 1
                            act.wait_ge(g_zs, n)
                            nc.scalar.activation(sig[0][:, 0, :], z[0][:, 0, :], ACT.Sigmoid).then_inc(g_sig, 1)
                            act.wait_ge(g_t, n)
                            nc.scalar.copy(act_T[0][:, 0:P], tp[:, 0:P]).then_inc(g_aT, 1)

                load_weights(act)
                nodes_act(act)
                all_stored(act, dst_stored)
                branches(act, general, windowed)
                update_act(act)

            @block.vector
            def _(dve):
                def windowed():
                    def hot_rows(c, k, round_end, first):
                        dve.wait_ge(dst_in[k], 16 * round_end)
                        if not first:
                            dve.wait_ge(z_done, 2 * c - 2)
                        nc.vector.tensor_scalar(lhs[k][WINDOW:P, :], dst_row[k][WINDOW:P, :],
                                                own_node[WINDOW:P, ds(c, 1)], None, ALU.is_equal) \
                            .then_inc(hotT_done, 1)

                    def hot_cols(c, k, first):
                        if not first:
                            dve.wait_ge(added, 2 * c - 2)
                            dve.wait_ge(count_done, c - 1)
                        nc.vector.tensor_tensor(
                            hot[k][:, :, :], iota_f[:, 0:WINDOW].unsqueeze(1).to_broadcast([P, TILES, WINDOW]),
                            drel[:, ds(c * TILES, TILES)].unsqueeze(2).to_broadcast([P, TILES, WINDOW]),
                            ALU.is_equal).then_inc(hot_done, 1)

                    def hot_sum(c, k, first):
                        dve.wait_ge(hot_done, c + 1)
                        if not first:
                            dve.wait_ge(added, 2 * c - 2)
                        with nc.allow_low_precision("counts up to 8 are exact"):
                            nc.vector.tensor_reduce(count[k][:, :], hot[k][:, :, :].rearrange("p t n -> p n t"), AX,
                                                    ALU.add).then_inc(count_done, 1)

                    def z_add(s, j, round_end, first):
                        b = j % 2
                        dve.wait_ge(z_done, s + 1)
                        dve.wait_ge(gathered[j], 64 * round_end)
                        if not first:
                            dve.wait_ge(sig_done, s - 1)
                            dve.wait_ge(a_done, s - 1)
                        nc.vector.tensor_tensor(
                            z[b][:, :, :], zp[b][:, :].rearrange("p (t c) -> p t c", t=HALF),
                            gath[j // 2][:, b * HALF:(b + 1) * HALF, :], ALU.add).then_inc(z_sum, 1)

                    def a_mul(s, j, first):
                        b = j % 2
                        dve.wait_ge(sig_done, s + 1)
                        if not first:
                            dve.wait_ge(tr_done, s - 1)
                        nc.vector.tensor_tensor(act_in[b][:, :, :], z[b][:, :, 0:D], sig[b][:, :, 0:D],
                                                ALU.mult).then_inc(a_done, 1)

                    def gate(s, j, first):
                        b = j % 2
                        dve.wait_ge(w2_done, s + 1)
                        dve.wait_ge(sig_done, s + 1)
                        if not first:
                            dve.wait_ge(added, s - 1)
                        nc.vector.tensor_tensor(msg[b][:, :, :], mp[b][:, :].rearrange("p (t c) -> p t c", t=HALF),
                                                sig[b][:, :, D:2 * D], ALU.mult).then_inc(msg_done, 1)

                    def add_window(c):
                        base = dve.value_load(base_i[0:1, ds(c, 1)], min_val=0, max_val=LAST_BASE)
                        to = sums[:, :, ds(base, WINDOW)]
                        dve.wait_ge(added, 2 * c + 2)
                        if not (isinstance(c, int) and c == 0):
                            dve.wait_ge(sums_done, c)
                        nc.vector.tensor_tensor(to, to, sp_[:, 0:2 * WINDOW].rearrange("p (k n) -> p k n", k=2),
                                                ALU.add).then_inc(sums_done, 1)

                    def steps(i, first=False, last=False):
                        for j in range(4):
                            s, c = 4 * i + j, 2 * i + j // 2
                            z_add(s, j, i + 1, first and j < 2)
                            if j == 1 or (j == 3 and not last):
                                hot_rows(c + 1, (j // 2 + 1) % 2, i + 1 + j // 2, first and j == 1)
                            if j % 2 == 0:
                                hot_cols(c, j // 2, first)
                            if j == 2 or (j == 0 and not first):
                                gate(s - 1, (j - 1) % 4, first and j <= 2)
                            a_mul(s, j, first and j < 2)
                            if j % 2 and not (first and j == 1):
                                add_window(c - 1)
                            if j % 2:
                                gate(s - 1, (j - 1) % 4, first and j <= 2)
                            if j % 2:
                                hot_sum(c, j // 2, first)

                    hot_rows(0, 0, 1, True)
                    steps(0, first=True)
                    with dve.Fori(1, ROUNDS - 1) as i:
                        steps(i)
                    steps(ROUNDS - 1, last=True)
                    gate(4 * ROUNDS - 1, 3, False)
                    add_window(CHUNKS - 1)
                    dve.wait_ge(sums_done, CHUNKS)

                def general():
                    with dve.Fori(0, CHUNKS) as c:
                        for t in range(TILES):
                            n = TILES * c + t + 1
                            dve.wait_ge(g_z, n)
                            dve.wait_ge(g_rows, 32 * n)
                            nc.vector.tensor_tensor(z[0][:, 1, :], zp[0][:, 0:2 * D], gath[0][:, 0, :], ALU.add) \
                                .then_inc(g_v, 1)
                            dve.wait_ge(g_v, (WIDES + 2) * (n - 1) + 1)
                            nc.vector.tensor_tensor(z[0][:, 0, :], z[0][:, 1, :], gath[0][:, 1, :], ALU.add) \
                                .then_inc(g_zs, 1)
                            dve.wait_ge(g_sig, n)
                            nc.vector.tensor_tensor(act_in[0][:, 0, :], z[0][:, 0, 0:D], sig[0][:, 0, 0:D], ALU.mult) \
                                .then_inc(g_a, 1)
                            dve.wait_ge(g_w2, n)
                            nc.vector.tensor_tensor(msg[0][:, 0, :], mp[0][:, 0:D], sig[0][:, 0, D:2 * D], ALU.mult) \
                                .then_inc(g_msg, 1)
                            nc.vector.tensor_copy(rel_w, dcol[:, ds(c * TILES + t, 1)]).then_inc(g_v, 1)
                            with dve.Fori(0, WIDES) as w:
                                done = (WIDES + 2) * (n - 1) + 2 + w
                                dve.wait_ge(g_v, done)
                                nc.vector.tensor_scalar(hot_w, iota_w, rel_w, None, ALU.is_equal).then_inc(g_hot, 1)
                                dve.wait_ge(g_hot, WIDES * (n - 1) + w + 1)
                                nc.vector.tensor_scalar(rel_w, rel_w, -float(WIDE), None, ALU.add).then_inc(g_v, 1)
                                dve.wait_ge(g_sum, WIDES * (n - 1) + w + 1)
                                to = sums[:, 0, ds(w * WIDE, WIDE)]
                                nc.vector.tensor_tensor(to, to, zp[1][:, 0:WIDE], ALU.add).then_inc(g_added, 1)
                                to = sums[:, 1, ds(w * WIDE, WIDE)]
                                nc.vector.tensor_tensor(to, to, zp[1][:, WIDE:2 * WIDE], ALU.add).then_inc(g_added, 1)
                                dve.wait_ge(g_added, 2 * (WIDES * (n - 1) + w + 1))
                            dve.wait_ge(g_v, (WIDES + 2) * n)
                            dve.sem_inc(g_start, 1)

                nodes_dve(dve)
                dve.wait_ge(h_tr, QUADS)
                dve.wait_ge(zeroed, 2)
                branches(dve, general, windowed)
                dve.sem_inc(edges_done, 1)
                update_dve(dve)

            @block.tensor
            def _(pe):
                def windowed():
                    def transposes(s, j, first):
                        pe.wait_ge(a_done, s + 1)
                        if not first:
                            pe.wait_ge(aT_done, s)
                        for t in range(HALF):
                            last = nc.tensor.transpose(tp[:, t * P:(t + 1) * P], act_in[j % 2][:, t, :], ident[:, :])
                        last.then_inc(tr_done, 1)

                    def z_products(s, c, j, round_end, first):
                        k, b = j // 2, j % 2
                        if b == 0:
                            pe.wait_ge(lhs_in[k], 32 * round_end)
                            pe.wait_ge(hotT_done, c + 1)
                        if not first:
                            pe.wait_ge(z_sum, s - 1)
                        for t in range(HALF):
                            e0 = (b * HALF + t) * P
                            last = nc.tensor.matmul(zp[b][:, t * 2 * D:(t + 1) * 2 * D], lhs[k][:, e0:e0 + P],
                                                    rhs[k][:, :], start=(t % 2 == 0), stop=True, skip_group_check=True)
                        last.then_inc(z_done, 1)

                    def w2_products(s, j, first):
                        b = j % 2
                        pe.wait_ge(aT_done, s + 1)
                        if not first:
                            pe.wait_ge(msg_done, s - 1)
                        elif s == 0:
                            pe.wait_ge(own_done, OWN_FILL)
                        bias(mp[b][:, :], 0, HALF * D)
                        for t in range(HALF):
                            last = nc.tensor.matmul(mp[b][:, t * D:(t + 1) * D], act_T[b][:, t * P:(t + 1) * P],
                                                    w2_sb, start=False, stop=True, skip_group_check=True)
                        last.then_inc(w2_done, 1)

                    def add_messages(s, c, j, first):
                        k, b = j // 2, j % 2
                        pe.wait_ge(msg_done, s + 1)
                        if b == 0:
                            pe.wait_ge(hot_done, c + 1)
                            if not first:
                                pe.wait_ge(sums_done, c)
                        for t in range(HALF):
                            last = nc.tensor.matmul(sp_[:, 0:WINDOW], msg[b][:, t, :], hot[k][:, b * HALF + t, :],
                                                    start=(b == 0 and t == 0), stop=True, skip_group_check=True)
                        if b == 1:
                            pe.wait_ge(count_done, c + 1)
                            last = nc.tensor.matmul(sp_[:, WINDOW:2 * WINDOW], ones_bf[:, :], count[k][:, :],
                                                    start=False, stop=True, skip_group_check=True)
                        last.then_inc(added, 1)

                    def steps(i, first):
                        for j in range(4):
                            s, c = 4 * i + j, 2 * i + j // 2
                            z_products(s, c, j, i + 1, first and j < 2)
                            if first and j == 1:
                                own_to_rows(pe, OWN_EARLY, OWN_FILL)
                            if not (first and j == 0):
                                transposes(s - 1, (j - 1) % 4, first and j == 1)
                            if not (first and j < 2):
                                add_messages(s - 2, c - 1, (j - 2) % 4, first)
                            if not (first and j == 0):
                                w2_products(s - 1, (j - 1) % 4, first and j <= 2)

                    steps(0, True)
                    with pe.Fori(1, ROUNDS) as i:
                        steps(i, False)
                    s = 4 * ROUNDS
                    pe.wait_ge(z_sum, s - 1)
                    own_products(OWN_FILL)
                    transposes(s - 1, 3, False)
                    add_messages(s - 2, CHUNKS - 1, 2, False)
                    w2_products(s - 1, 3, False)
                    own_products(OWN_FILL + 1)
                    add_messages(s - 1, CHUNKS - 1, 3, False)
                    pe.wait_ge(z_sum, s)
                    for q in range(OWN_FILL + 2, QUADS):
                        own_products(q)

                def general():
                    own_to_rows(pe, OWN_EARLY, OWN_FILL)
                    pe.wait_ge(own_done, OWN_FILL)
                    with pe.Fori(0, CHUNKS) as c:
                        pe.wait_ge(g_in, 48 * (c + 1))
                        for t in range(TILES):
                            n = TILES * c + t + 1
                            pe.wait_ge(g_start, n)
                            nc.tensor.matmul(zp[0][:, 0:2 * D], lhs[0][0:ED, t * P:(t + 1) * P], rhs[0][0:ED, :],
                                             start=True, stop=True).then_inc(g_z, 1)
                            pe.wait_ge(g_a, n)
                            nc.tensor.transpose(tp[:, 0:P], act_in[0][:, 0, :], ident[:, :]).then_inc(g_t, 1)
                            pe.wait_ge(g_aT, n)
                            bias(mp[0][:, 0:D], 0, D)
                            nc.tensor.matmul(mp[0][:, 0:D], act_T[0][:, 0:P], w2_sb, start=False, stop=True,
                                             skip_group_check=True) \
                                .then_inc(g_w2, 1)
                            pe.wait_ge(g_msg, n)
                            pe.sem_inc(g_windows, 1)
                            with pe.Fori(0, WIDES) as w:
                                pe.wait_ge(g_hot, WIDES * (n - 1) + w + 1)
                                nc.tensor.matmul(zp[1][:, 0:WIDE], msg[0][:, 0, :], hot_w, start=True, stop=True)
                                nc.tensor.matmul(zp[1][:, WIDE:2 * WIDE], ones[:, :], hot_w, start=True, stop=True) \
                                    .then_inc(g_sum, 1)
                    pe.wait_ge(edges_done, 1)
                    for q in range(OWN_FILL, QUADS):
                        own_products(q)

                nodes_pe(pe)
                pe.wait_ge(staged_dst, QUADS)
                branches(pe, general, windowed)
                update_pe(pe)


def kernel(**inputs):
    import numpy as np
    import concourse.bacc as bacc
    from concourse.bass_utils import run_bass_kernel_spmd as run

    edge = np.concatenate([np.arange((CHUNKS - 1) * CHUNK), np.arange(E - CHUNK, E)])
    src = np.asarray(inputs["src"])[edge].reshape(CHUNKS, TILES, P)
    dst = np.asarray(inputs["dst"])[edge].reshape(CHUNKS, TILES, P)
    e = np.asarray(inputs["edge_attr_64"])[edge].reshape(CHUNKS, CHUNK, ED)
    weight = {k: np.asarray(inputs["L0_gnn_" + k]) for k in ("w1", "b1", "w2", "b2", "wg", "bg", "wu", "bu")}
    arrays = {
        "x": inputs["x"],
        "src_ch": src.transpose(0, 2, 1),
        "dst_rows": dst.reshape(CHUNKS, CHUNK),
        "dst_cols": dst.transpose(2, 0, 1).reshape(P, CHUNKS * TILES),
        "dst_first": dst[:, 0, 0].reshape(1, CHUNKS),
        "e_ch": e.transpose(0, 2, 1),
        "w_z": np.concatenate([weight["w1"], weight["wg"]], axis=1),
        "w_sq": np.concatenate([weight["w2"], weight["wu"]], axis=0),
        "biases": np.concatenate([weight[k] for k in ("b1", "bg", "b2", "bu")])[None],
    }
    nc = bacc.Bacc("TRN2", target_bir_lowering=False, num_devices=1)
    args, maps = [], {}
    for name, a in arrays.items():
        a = np.ascontiguousarray(a)
        maps[f"in_{name}"] = a
        args.append(nc.dram_tensor(f"in_{name}", a.shape, mybir.dt.from_np(a.dtype), kind="ExternalInput").ap())
    args.append(nc.dram_tensor("out", (N, D), mybir.dt.float32, kind="ExternalOutput").ap())
    gnn_program(nc, *args)
    return run(nc, [maps], core_ids=[0]).results[0]["out"]
```
